# Optimizing a Trainium2 kernel written in Bass

```python
import numpy as np
import jax
import jax.numpy as jnp

def _softmax(x, axis=-1):
    return jax.nn.softmax(x, axis=axis)

def _gelu(x):
    return jax.nn.gelu(x, approximate=True)

def _silu(x):
    return jax.nn.silu(x)

def _sigmoid(x):
    return jax.nn.sigmoid(x)

def _layernorm(x, axis=-1, eps=1e-05):
    m = jnp.mean(x, axis=axis, keepdims=True)
    v = jnp.var(x, axis=axis, keepdims=True)
    return (x - m) / jnp.sqrt(v + eps)

def _scatter_add(tgt, idx, src, axis=0):
    return tgt.at[idx].add(src)

def _segment_sum(src, seg, n):
    return jax.ops.segment_sum(src, seg, n)
kernel_name = 'mk_decoder_postln_d1_seqx_r4_9f4146'

def setup_inputs(seed: int=0):
    np.random.seed(seed)
    _w = jnp.asarray

    def _rec_inputs():
        import jax
        import jax.numpy as jnp
        _rk = jax.random.key(seed)
        x = 7.22e-05 + 1 * jax.random.normal(jax.random.fold_in(_rk, 1), (8, 512, 256), jnp.float32)
        _lenS = 512 - jax.random.randint(jax.random.fold_in(_rk, 7), (8,), 0, max(1, 512 // 4) + 1, jnp.int32)
        _lenS2 = 512 - jax.random.randint(jax.random.fold_in(_rk, 8), (8,), 0, max(1, 512 // 4) + 1, jnp.int32)
        _ctx_1024P = jax.random.normal(jax.random.fold_in(_rk, 11), (8, 16, 256), jnp.float32)
        _ctx_1024c = jax.random.dirichlet(jax.random.fold_in(_rk, 511), 0.3 * jnp.ones((16,), jnp.float32), (8, 512))
        _ctx_1024t = jnp.einsum('bsk,bkd->bsd', _ctx_1024c, _ctx_1024P)
        _ctx_1024t = _ctx_1024t * jax.lax.rsqrt(jnp.mean(jnp.square(_ctx_1024t)) + 1e-12) * 0.953939
        ctx_1024 = 4.13588e-05 + 0.999923 * (_ctx_1024t + 0.3 * jax.random.normal(jax.random.fold_in(_rk, 611), (8, 512, 256), jnp.float32))
        fside_BxSxS2_0 = -1.47943e-05 + 1.00017 * jax.random.normal(jax.random.fold_in(_rk, 12), (8, 512, 512), jnp.float32)
        return (x, ctx_1024, fside_BxSxS2_0)
    x, ctx_1024, fside_BxSxS2_0 = _rec_inputs()

    def _L0_attn_setup():
        import jax, jax.numpy as jnp
        import numpy as np
        LN_EPS = 1e-05
        NUM_HEAD = 16
        key = jax.random.key(seed)
        ks = jax.random.split(key, 10)
        B, S, E = (2, 512, 256)
        sc = 0.02
        return {'x': jax.random.normal(ks[0], (B, S, E), jnp.float32), 'wq': jax.random.normal(ks[1], (E, E), jnp.float32) * sc, 'bq': jax.random.normal(ks[2], (E,), jnp.float32) * sc, 'wk': jax.random.normal(ks[3], (E, E), jnp.float32) * sc, 'bk': jax.random.normal(ks[4], (E,), jnp.float32) * sc, 'wv': jax.random.normal(ks[5], (E, E), jnp.float32) * sc, 'bv': jax.random.normal(ks[6], (E,), jnp.float32) * sc, 'wo': jax.random.normal(ks[7], (E, E), jnp.float32) * sc, 'bo': jax.random.normal(ks[8], (E,), jnp.float32) * sc, 'gamma': jnp.ones((E,), jnp.float32), 'beta': jnp.zeros((E,), jnp.float32)}
    _L0_attn_all = _L0_attn_setup()
    _L0_attn_in = {k: v for k, v in _L0_attn_all.items() if k in ('wq', 'bq', 'wk', 'bk', 'wv', 'bv', 'wo', 'bo', 'gamma', 'beta')}
    del _L0_attn_all

    def _L0_xattn_setup():
        import jax, jax.numpy as jnp
        import numpy as np
        D = 256
        key = jax.random.key(seed)
        ks = jax.random.split(key, 13)
        B, S, d = (4, 512, D)
        inp = {'q_in': jax.random.normal(ks[0], (B, S, d), jnp.float32), 'k_in': jax.random.normal(ks[1], (B, S, d), jnp.float32), 'v_in': jax.random.normal(ks[2], (B, S, d), jnp.float32), 'phi_risk': jax.random.normal(ks[3], (B, S, S), jnp.float32), 'phi_prio': jax.random.normal(ks[4], (B, S, S), jnp.float32), 'phi_impl': jax.random.normal(ks[5], (B, S, S), jnp.float32), 'Wq': jax.random.normal(ks[6], (d, d), jnp.float32) / np.sqrt(d), 'bq': jax.random.normal(ks[7], (d,), jnp.float32) * 0.01, 'Wk': jax.random.normal(ks[8], (d, d), jnp.float32) / np.sqrt(d), 'bk': jax.random.normal(ks[9], (d,), jnp.float32) * 0.01, 'Wv': jax.random.normal(ks[10], (d, d), jnp.float32) / np.sqrt(d), 'bv': jax.random.normal(ks[11], (d,), jnp.float32) * 0.01, 'beta_risk': jnp.float32(0.1), 'beta_prio': jnp.float32(0.1), 'beta_impl': jnp.float32(0.1)}
        return inp
    _L0_xattn_all = _L0_xattn_setup()
    _L0_xattn_in = {k: v for k, v in _L0_xattn_all.items() if k in ('Wq', 'bq', 'Wk', 'bk', 'Wv', 'bv', 'beta_risk', 'beta_prio', 'beta_impl')}
    del _L0_xattn_all

    def _L0_ffn_setup():
        import jax, jax.numpy as jnp
        import numpy as np
        TOP_K = 2
        key = jax.random.key(seed)
        ks = jax.random.split(key, 6)
        B, T, H, E, F = (2, 512, 256, 8, 1024)
        s = 0.02
        return {'hidden_states': jax.random.normal(ks[0], (B, T, H), dtype=jnp.float32), 'router_w': jax.random.normal(ks[1], (E, H), dtype=jnp.float32) * s, 'w1': jax.random.normal(ks[2], (E, F, H), dtype=jnp.float32) * s, 'b1': jax.random.normal(ks[3], (E, F), dtype=jnp.float32) * s, 'w2': jax.random.normal(ks[4], (E, H, F), dtype=jnp.float32) * s, 'b2': jax.random.normal(ks[5], (E, H), dtype=jnp.float32) * s}
    _L0_ffn_all = _L0_ffn_setup()
    _L0_ffn_in = {k: v for k, v in _L0_ffn_all.items() if k in ('router_w', 'w1', 'b1', 'w2', 'b2')}
    del _L0_ffn_all
    return {'x': x, 'ctx_1024': ctx_1024, 'fside_BxSxS2_0': fside_BxSxS2_0, 'L0_attn_wq': _L0_attn_in['wq'], 'L0_attn_bq': _L0_attn_in['bq'], 'L0_attn_wk': _L0_attn_in['wk'], 'L0_attn_bk': _L0_attn_in['bk'], 'L0_attn_wv': _L0_attn_in['wv'], 'L0_attn_bv': _L0_attn_in['bv'], 'L0_attn_wo': _L0_attn_in['wo'], 'L0_attn_bo': _L0_attn_in['bo'], 'L0_attn_gamma': _L0_attn_in['gamma'], 'L0_attn_beta': _L0_attn_in['beta'], 'L0_xattn_Wq': _L0_xattn_in['Wq'], 'L0_xattn_bq': _L0_xattn_in['bq'], 'L0_xattn_Wk': _L0_xattn_in['Wk'], 'L0_xattn_bk': _L0_xattn_in['bk'], 'L0_xattn_Wv': _L0_xattn_in['Wv'], 'L0_xattn_bv': _L0_xattn_in['bv'], 'L0_xattn_beta_risk': _L0_xattn_in['beta_risk'], 'L0_xattn_beta_prio': _L0_xattn_in['beta_prio'], 'L0_xattn_beta_impl': _L0_xattn_in['beta_impl'], 'L0_ffn_router_w': _L0_ffn_in['router_w'], 'L0_ffn_w1': _L0_ffn_in['w1'], 'L0_ffn_b1': _L0_ffn_in['b1'], 'L0_ffn_w2': _L0_ffn_in['w2'], 'L0_ffn_b2': _L0_ffn_in['b2']}

def reference(x, ctx_1024, fside_BxSxS2_0, L0_attn_wq, L0_attn_bq, L0_attn_wk, L0_attn_bk, L0_attn_wv, L0_attn_bv, L0_attn_wo, L0_attn_bo, L0_attn_gamma, L0_attn_beta, L0_xattn_Wq, L0_xattn_bq, L0_xattn_Wk, L0_xattn_bk, L0_xattn_Wv, L0_xattn_bv, L0_xattn_beta_risk, L0_xattn_beta_prio, L0_xattn_beta_impl, L0_ffn_router_w, L0_ffn_w1, L0_ffn_b1, L0_ffn_w2, L0_ffn_b2):
    import jax
    import jax.numpy as jnp

    def _L0_attn_ref(x, wq, bq, wk, bk, wv, bv, wo, bo, gamma, beta):
        import jax, jax.numpy as jnp
        import numpy as np
        LN_EPS = 1e-05
        NUM_HEAD = 16
        B, S, E = x.shape
        H = NUM_HEAD
        D = E // H
        Q = x @ wq + bq
        K = x @ wk + bk
        V = x @ wv + bv
        Q = Q.reshape(B * H, S, D)
        K = K.reshape(B * H, S, D)
        V = V.reshape(B * H, S, D)
        scores = jnp.einsum('bqd,bkd->bqk', Q, K) / jnp.sqrt(jnp.float32(D))
        attn = jax.nn.softmax(scores, axis=-1)
        ctx = jnp.einsum('bqk,bkd->bqd', attn, V)
        ctx = ctx.reshape(B, S, E)
        out = ctx @ wo + bo
        out = out + x
        mu = jnp.mean(out, axis=-1, keepdims=True)
        var = jnp.var(out, axis=-1, keepdims=True)
        out = (out - mu) * jax.lax.rsqrt(var + LN_EPS) * gamma + beta
        return out

    def _L0_xattn_ref(q_in, k_in, v_in, phi_risk, phi_prio, phi_impl, Wq, bq, Wk, bk, Wv, bv, beta_risk, beta_prio, beta_impl):
        import jax, jax.numpy as jnp
        import numpy as np
        D = 256
        d = q_in.shape[-1]
        scale = jnp.asarray(d, q_in.dtype) ** (-0.5)
        Q = q_in @ Wq.T + bq
        K = k_in @ Wk.T + bk
        V = v_in @ Wv.T + bv
        att = jnp.einsum('bsd,btd->bst', Q, K) * scale
        att = att + beta_risk * phi_risk + beta_prio * phi_prio - beta_impl * phi_impl
        w = jax.nn.softmax(att, axis=-1)
        return jnp.einsum('bst,btd->bsd', w, V)

    def _L0_ffn_ref(hidden_states, router_w, w1, b1, w2, b2):
        import jax, jax.numpy as jnp
        import numpy as np
        TOP_K = 2
        x = hidden_states
        router_logits = jnp.einsum('bth,eh->bte', x, router_w)
        topk_values, topk_indices = jax.lax.top_k(router_logits, TOP_K)
        topk_weights = jax.nn.softmax(topk_values.astype(jnp.float32), axis=-1).astype(x.dtype)
        h1 = jnp.einsum('bth,efh->btef', x, w1) + b1
        h1 = jax.nn.gelu(h1, approximate=False)
        expert_outputs = jnp.einsum('btef,ehf->bteh', h1, w2) + b2
        gather_idx = topk_indices[..., None]
        topk_expert_outputs = jnp.take_along_axis(expert_outputs, gather_idx, axis=2)
        mixed_output = jnp.sum(topk_expert_outputs * topk_weights[..., None], axis=2)
        return mixed_output
    x = _layernorm(x + _L0_attn_ref(x, L0_attn_wq, L0_attn_bq, L0_attn_wk, L0_attn_bk, L0_attn_wv, L0_attn_bv, L0_attn_wo, L0_attn_bo, L0_attn_gamma, L0_attn_beta), axis=-1)
    x = _layernorm(x + _L0_xattn_ref(x, ctx_1024, ctx_1024, fside_BxSxS2_0, fside_BxSxS2_0, fside_BxSxS2_0, L0_xattn_Wq, L0_xattn_bq, L0_xattn_Wk, L0_xattn_bk, L0_xattn_Wv, L0_xattn_bv, L0_xattn_beta_risk, L0_xattn_beta_prio, L0_xattn_beta_impl), axis=-1)
    x = _layernorm(x + _L0_ffn_ref(x, L0_ffn_router_w, L0_ffn_w1, L0_ffn_b1, L0_ffn_w2, L0_ffn_b2), axis=-1)
    return x

_drawn_inputs = setup_inputs


def setup_inputs(seed=0):
    import zlib

    import numpy as np

    out = dict(_drawn_inputs(seed))
    spreads = {'L0_attn_gamma': (1.0, 0.2), 'L0_attn_beta': (0.0, 0.1)}
    factors = {'fside_BxSxS2_0': 7.779,
     'L0_attn_wq': 8.0,
     'L0_attn_bq': 8.0,
     'L0_attn_wk': 8.0,
     'L0_attn_bk': 8.0,
     'L0_attn_wv': 8.0,
     'L0_attn_bv': 8.0,
     'L0_attn_wo': 8.0,
     'L0_attn_bo': 18.269,
     'L0_xattn_bq': 27.168,
     'L0_xattn_bk': 64.0,
     'L0_xattn_bv': 5.149,
     'L0_ffn_b1': 8.0,
     'L0_ffn_b2': 3.862}
    for name, (base, spread) in spreads.items():
        noise = np.random.default_rng([zlib.crc32(name.encode()), seed]).standard_normal(out[name].shape)
        drawn = base * np.exp(spread * noise) if base else spread * noise
        out[name] = jnp.asarray(drawn.astype(out[name].dtype))
    for name, factor in factors.items():
        out[name] = (out[name] * factor).astype(out[name].dtype)
    return out
```

```python
from contextlib import ExitStack

import concourse.bass as bass
from concourse import mybir

F32 = mybir.dt.float32
BF16 = mybir.dt.bfloat16
FP16 = mybir.dt.float16
I32 = mybir.dt.int32
U32 = mybir.dt.uint32
ALU = mybir.AluOpType
ACT = mybir.ActivationFunctionType
AX = mybir.AxisListType

P = 128
E = 256
ET = E // P
HEADS = 4
HT = 32
G = 16
D = 16
S = 512
NJ = S // P
B = 8
T = B * S
UNITS = T // P
QB = S // P
TERMS = 6
KROWS = TERMS * D
VW = 50
NE = 8
FF = 1024
FC = FF // P
REGION = T + P
XW = E + 2
TILES = (2 * T + NE * (P - 1)) // P + 1
TILES += -TILES % 4
DUMP = 2 * T
EPS = 1e-5


class Count:

    def __init__(self, base, mul, add):
        self.base, self.mul, self.add = base, mul, add

    def __add__(self, k):
        return Count(self.base, self.mul, self.add + k)

    def __sub__(self, k):
        return self + -k

    def __mul__(self, k):
        return Count(self.base, self.mul * k, self.add * k)

    __rmul__ = __mul__


def at(count):
    if not isinstance(count, Count):
        return count
    return count.add if isinstance(count.base, int) else count.base * count.mul + count.add


class Unit:

    def __init__(self, base, off, total=UNITS):
        self.base, self.off, self.total = base, off, total
        self.r = off % 4
        self.n = Count(base, 4, off)
        self.b = Count(base, 1, off // 4)

    def plus(self, k):
        return Unit(self.base, self.off + k, self.total)

    def fixed(self):
        return isinstance(self.base, int)

    def real(self):
        return not self.fixed() or 0 <= self.off < self.total

    def among_first(self, k):
        return self.fixed() and self.off < k

    def first(self):
        return self.among_first(1)


def build_decoder(nc, a, out):
    ctx = ExitStack()
    with ctx:
        def sb(name, shape, dt):
            return ctx.enter_context(nc.sbuf_tensor("b_" + name, shape, dt))

        def ps(name, shape, dt):
            return ctx.enter_context(nc.psum_tensor("p_" + name, shape, dt))

        def sem(name):
            return ctx.enter_context(nc.semaphore("s_" + name))

        sorted_x = nc.dram_tensor("sorted_x", (NE * REGION + P, XW), F32).ap()
        results = nc.dram_tensor("results", (2 * T + P, E), F32).ap()
        x2_dram = nc.dram_tensor("x2_dram", (UNITS, P, E), F32).ap()

        identf = sb("identf", [P, P], F32)
        identb = sb("identb", [P, P], BF16)
        before = sb("before", [P, P], BF16)
        onesb = sb("onesb", [P, P], BF16)
        iota8 = sb("iota8", [P, NE], F32)
        ids = sb("ids", [P, 2], F32)
        half = sb("half", [P, 1], F32)
        bo = sb("bo", [P, E], F32)
        gamma = sb("gamma", [P, E], F32)
        beta = sb("beta", [P, E], F32)
        bqx = sb("bqx", [P, ET], F32)
        bkx = sb("bkx", [P, ET], F32)
        bvx = sb("bvx", [P, E], F32)
        betas = sb("betas", [P, 3], F32)
        coef = sb("coef", [P, 2], F32)
        rw = sb("rw", [P, ET, NE], F32)

        arena2 = sb("arena2", [P, NE * FC * E], F32)
        arena1 = sb("arena1", [P, NE * ET * FF], F32)
        arenaf = sb("arenaf", [P, 2 * ET * FF], F32)
        carved = {"b_arena2": 0, "b_arena1": 0, "b_arenaf": 0}

        def carve(words, arena=arena2):
            carved[arena.name] += words
            return arena[:, carved[arena.name] - words:carved[arena.name]]

        def square(t):
            return t.rearrange("p (e n) -> p e n", e=ET)

        prob = carve(HEADS * NJ * S)
        prob_hi = prob.bitcast(BF16)
        low = carve(HEADS * NJ * S // 2).bitcast(FP16)
        qs = [carve(HEADS * S // 2).bitcast(BF16) for _ in range(4)]
        w2 = arena2[:, :].rearrange("p (e c n) -> p e c n", e=NE, c=FC)
        wqkv = square(carve(ET * 3 * E, arena1))
        bqkv = carve(3 * E, arena1)
        q32 = carve(3 * E, arena1)
        xq = carve(G * TERMS * D // 2, arena1).bitcast(BF16).rearrange("p (g a d) -> p g a d", g=G, a=TERMS)
        xk = carve(G * TERMS * D // 2, arena1).bitcast(BF16).rearrange("p (g a d) -> p g a d", g=G, a=TERMS)
        xv = carve(G * VW // 2, arena1).bitcast(BF16).rearrange("p (g w) -> p g w", g=G)
        xt = carve(4 * E, arena1).rearrange("p (u e t) -> p u e t", u=4, e=ET)
        ct = carve(4 * E, arena1).rearrange("p (u e t) -> p u e t", u=4, e=ET)
        ks = [carve(HEADS * S // 2, arena1).bitcast(BF16) for _ in range(4)]
        vs = carve(4 * HEADS * NJ * VW // 2, arena1).bitcast(BF16).rearrange("p (u h w) -> p u h w", u=4, h=HEADS)
        wo = square(carve(ET * E, arenaf))
        wqx = square(carve(ET * E, arenaf))
        wkx = square(carve(ET * E, arenaf))
        wvx = square(carve(ET * E, arenaf))
        phs = carve(S, arenaf)
        att = carve(S, arenaf)
        p5 = carve(S, arenaf)
        p5t = carve(S, arenaf).rearrange("p (j t) -> p j t", j=QB)
        xin = sb("xin", [P, 4, E], F32)
        phi = sb("phi", [P, 4, S], F32)
        nmx = sb("nmx", [P, 2, 16], F32)
        xm = sb("xm", [P, 3, 16], BF16)
        xmr = sb("xmr", [P, 2, 16], F32)
        mrow = sb("mrow", [P, P], BF16)
        psums = sb("psums", [P, 8, D], F32)
        prec = sb("prec", [P, 8], F32)
        cx = sb("cx", [P, HEADS * 64], F32)
        cxt = sb("cxt", [P, ET, P], F32)
        xb = sb("xb", [P, 2, E], F32)
        y1 = sb("y1", [P, E], F32)
        z1 = sb("z1", [P, E], F32)
        st = sb("st", [P, 3, 6], F32)
        mv = sb("mv", [P, 3, 2], F32)
        ve = sb("ve", [P, 3], F32)
        rs = sb("rs", [P, 3], F32)
        x1 = sb("x1", [P, 2, E], F32)
        x1t = sb("x1t", [P, ET, P], F32)
        qxt = sb("qxt", [P, ET, P], F32)
        kx = sb("kx", [P, 2 * ET * S], F32)
        vx = sb("vx", [P, 2 * QB * E], F32)
        nmx5 = sb("nmx5", [P, 2], F32)
        sum5 = sb("sum5", [P, 2], F32)
        y2 = sb("y2", [P, E], F32)
        pl = sb("pl", [P, 2, 2, XW], F32)
        x2t = sb("x2t", [P, ET, P], F32)
        lg = sb("lg", [P, NE], F32)
        top = sb("top", [P, 8], F32)
        topi = sb("topi", [P, 8], U32)
        topf = sb("topf", [P, 2], F32)
        oh = sb("oh", [P, 2, NE], F32)
        chosen = sb("chosen", [P, NE], BF16)
        gate = sb("gate", [P, 3], F32)
        base = sb("base", [P, NE], F32)
        ohb = sb("ohb", [P, 2, NE], F32)
        slotf = sb("slotf", [P, 2], F32)
        slot = sb("slot", [P, 2, 2], U32)
        cnt = sb("cnt", [P, NE], F32)

        w1 = arena1
        b1 = sb("b1", [P, NE * FC], F32)
        b2 = phi[:, :, :].rearrange("p u s -> p (u s)")
        pad = sb("pad", [P, XW], F32)
        iotap = sb("iotap", [P, 2], F32)
        starts = sb("starts", [P, NE], F32)
        padf = sb("padf", [P, NE], F32)
        padto = sb("padto", [P, NE], U32)
        cnt_i = sb("cnt_i", [1, 2, NE], I32)
        plan = sb("plan", [1, 4, NE], F32)
        tiles = sb("tiles", [1, TILES], F32)
        past = kx[0:1, 0:TILES * NE].rearrange("p (t e) -> p t e", e=NE)
        jump = kx[0:1, TILES * NE:2 * TILES * NE].rearrange("p (t e) -> p t e", e=NE)
        tabf = sb("tabf", [1, 3, TILES], F32)
        table = sb("table", [1, 2, TILES], I32)
        xg = sb("xg", [P, 4, XW], F32)
        w1f = arenaf[:, :].rearrange("p (a f) -> p a f", a=2)
        xgt = x1t, x2t
        hidden = [kx[:, 0:FC * P], kx[:, FC * P:2 * FC * P]]
        bw = sb("bw", [P, E], F32)
        yo = vx[:, 0:2 * E].rearrange("p (a e) -> p a e", a=2)
        res = phi[:, :, :]
        x2in = xin
        tot = arena2[:, 0:4 * E].rearrange("p (u e) -> p u e", u=4)
        fst = sb("fst", [P, 4, 6], F32)
        fmv = sb("fmv", [P, 4, 2], F32)
        fve = sb("fve", [P, 4], F32)
        frs = sb("frs", [P, 4], F32)
        fout = arena2[:, 4 * E:8 * E].rearrange("p (u e) -> p u e", u=4)

        pm = ps("pm", [P, 2, S], F32)
        pe_ = ps("pe", [P, 2, S], F32)
        pv = ps("pv", [P, 2, S], F32)
        pz = ps("pz", [P, 2, S], F32)

        def zb(bank):
            return pz[:, bank, :].bitcast(BF16)

        s_w = sem("weights_loaded")
        s_k = sem("constants_made")
        s_c2 = sem("coef_made")
        s_xt = [sem(f"xt_loaded{g}") for g in range(4)]
        s_xp = [sem(f"x_phi_loaded{g}") for g in range(4)]
        s_pqk = sem("proj_qk_done")
        s_pvv = sem("proj_v_done")
        s_q32 = sem("q32_written")
        s_h = sem("high_parts")
        s_r = sem("first_rest")
        s_m = sem("middle_parts")
        s_xv = sem("value_parts")
        s_rep = sem("parts_replicated")
        s_tr = sem("stack_transposed")
        s_stk = sem("stack_written")
        s_vs = [sem(f"values_moved{g}") for g in range(4)]
        s_mxq = sem("max_scores")
        s_red = sem("max_reduced")
        s_xm = sem("max_parts")
        s_mt = sem("max_transposed")
        s_mrow = sem("max_row_written")
        s_mr = [sem(f"max_rows_moved{g}") for g in range(4)]
        s_qkt = sem("exp_scores")
        s_exp = sem("exp_written")
        s_lo = sem("low_written")
        s_pv = sem("values_summed")
        s_vsum = sem("value_bank_read")
        s_c = sem("context_written")
        s_ctr = sem("context_transposed")
        s_ct = sem("context_t_written")
        s_o = sem("o_proj_done")
        s_xb = sem("x_plus_bias")
        s_l1 = sem("ln1_steps")
        s_l2 = sem("ln2_steps")
        s_rs1 = sem("rstd1")
        s_rs2 = sem("rstd2")
        s_x1 = sem("x1_written")
        s_x1t = sem("x1_transposed")
        s_x1te = sem("x1t_written")
        s_qt = sem("qx_done")
        s_qte = sem("qx_written")
        s_kt = sem("kx_done")
        s_kte = sem("kx_written")
        s_vt = sem("vx_done")
        s_vte = sem("vx_written")
        s_ph = sem("phi_scaled")
        s_s = sem("cross_scores")
        s_t = sem("cross_max")
        s_e5 = sem("cross_exp")
        s_pt = sem("cross_p_transposed")
        s_pte = sem("cross_pt_written")
        s_pv5 = sem("cross_values")
        s_l5 = sem("ln5_steps")
        s_rs5 = sem("rstd5")
        s_x2 = sem("x2_written")
        s_pl2 = sem("x2_second_copy")
        s_x2d = [sem(f"x2_stored{g}") for g in range(2)]
        s_x2t = sem("x2_transposed")
        s_x2te = sem("x2t_written")
        s_rt = sem("router_done")
        s_rc = sem("choice_steps")
        s_e2 = sem("gate_exp")
        s_pf = sem("prefix_done")
        s_rd = sem("slot_steps")
        s_sc = [sem(f"rows_scattered{g}") for g in range(2)]

        s_w1 = sem("w1_loaded")
        s_w2 = sem("w2_loaded")
        s_b = sem("expert_biases_loaded")
        s_pad = sem("pad_steps")
        s_padd = sem("pads_written")
        s_plan = sem("plan_steps")
        s_tab = sem("table_written")
        s_fx = [sem(f"tile_loaded{g}") for g in range(4)]
        s_ft = sem("tile_transposed")
        s_fxt = sem("tile_t_written")
        s_fw = sem("w1_fetched")
        s_fh = sem("hidden_banks")
        s_fg = sem("gelu_banks")
        s_fy = sem("expert_out")
        s_fb = sem("bias_weighted")
        s_fo = sem("result_written")
        s_fs = sem("results_scattered")
        s_rl = [sem(f"results_loaded{g}") for g in range(4)]
        s_ra = sem("results_added")
        s_ln = sem("last_ln_steps")
        s_lr = sem("last_rstd")
        s_ly = sem("output_written")
        s_lo_ = [sem(f"output_stored{g}") for g in range(4)]

        block = ctx.enter_context(nc.Block())

        loads = [
            (wqkv[:], a["wqkv"]), (wo[:], a["wo"]), (wqx[:], a["wqx"]), (wkx[:], a["wkx"]), (wvx[:], a["wvx"]),
            (rw[:], a["rw"]), (bqkv[:], a["bqkv"].partition_broadcast(P)), (bo[:], a["bo"].partition_broadcast(P)),
            (gamma[:], a["gamma"].partition_broadcast(P)), (beta[:], a["beta"].partition_broadcast(P)),
            (bvx[:], a["bvx"].partition_broadcast(P)), (bqx[:], a["bqx"]), (bkx[:], a["bkx"]),
            (betas[:, 0:1], a["beta_risk"].partition_broadcast(P)),
            (betas[:, 1:2], a["beta_prio"].partition_broadcast(P)),
            (betas[:, 2:3], a["beta_impl"].partition_broadcast(P)),
        ]
        NLOADS = 16 * len(loads)
        NCONST = 16

        LEADS = dict(front=3, peak=2, row=1, soft=0, attn=-1, cross=-2, route=-3, place=-4)

        def stages(i):
            return {name: Unit(i.base[name] if i.looped else 0, i.off + lead) for name, lead in LEADS.items()}

        class Iteration:

            def __init__(self, base, off):
                self.base, self.off, self.looped = base, off, base is not None

        def own(eng, b, most=6):
            copy = eng.alloc_register(f"stage_base{nc.next_id()}")
            eng.reg_mov(copy, b)
            return eng.snap(copy, min_val=1, max_val=most)

        def run(eng, iteration):
            for n in range(-3, 4):
                iteration(stages(Iteration(None, n)), False)
            with eng.Fori(1, 7) as b:
                base = {name: own(eng, b) for name in LEADS}
                for r in range(4):
                    iteration(stages(Iteration(base, r)), r == 0)
            for n in range(28, 36):
                iteration(stages(Iteration(None, n)), n == 28)

        def run_tiles(eng, iteration):
            for n in range(-1, 4):
                iteration(Unit(0, n, TILES))
            with eng.Fori(1, TILES // 4 - 1) as b:
                base = own(eng, b, TILES // 4 - 2)
                for r in range(4):
                    iteration(Unit(base, r, TILES))
            for n in range(TILES - 4, TILES + 1):
                iteration(Unit(0, n, TILES))

        def run_last(eng, iteration):
            for n in range(4):
                iteration(Unit(0, n))
            with eng.Fori(1, UNITS // 4) as b:
                base = own(eng, b, UNITS // 4 - 1)
                for r in range(4):
                    iteration(Unit(base, r))
            iteration(Unit(0, UNITS))

        @block.sync
        def _(sp):
            with nc.allow_non_contiguous_dma(reason="bias columns"):
                for dst, src in loads:
                    sp.dma_start(dst, src).then_inc(s_w, 16)


            def load_t(u):
                if not u.real():
                    return
                if not (u.among_first(4)):
                    sp.wait_ge(s_vt, at(u.n - 3))
                sp.dma_start(xt[:, u.r], a["xt"][bass.ds(at(u.n), 1)].rearrange("o p e t -> p (o e) t")).then_inc(s_xt[u.r], 16)
                sp.dma_start(ct[:, u.r], a["ct"][bass.ds(at(u.n), 1)].rearrange("o p e t -> p (o e) t")).then_inc(s_xt[u.r], 16)

            def iteration(st_, _):
                load_t(st_["front"].plus(1))
                i = st_["soft"]
                if i.real():
                    if not (i.among_first(4)):
                        sp.wait_ge(s_ph, at(i.n - 3))
                    sp.dma_start(xin[:, i.r], a["x"][bass.ds(at(i.n), 1)].rearrange("o t e -> (o t) e")).then_inc(s_xp[i.r], 16)
                    sp.dma_start(phi[:, i.r], a["phi"][bass.ds(at(i.n), 1)].rearrange("o t e -> (o t) e")).then_inc(s_xp[i.r], 16)
                u = st_["row"]
                if u.real():
                    sp.wait_ge(s_mrow, at(u.n + 1))
                    for t in range(3):
                        sp.dma_start(qs[u.r][KROWS + t:KROWS + t + 1, :].rearrange("o (m q) -> o m q", q=P),
                                     mrow[16 * t:16 * t + 16, :]).then_inc(s_mr[u.r], 16)
                u = st_["route"]
                if u.real():
                    sp.wait_ge(s_x2, at(u.n + 1))
                    sp.dma_start(x2_dram[bass.ds(at(u.n), 1)].rearrange("o t e -> (o t) e"), pl[:, u.r % 2, 0, 0:E]).then_inc(s_x2d[u.r % 2], 16)
                u = st_["front"]
                if u.real():
                    sp.wait_ge(s_xv, at(u.n + 1))
                    sp.nop(nofuse=True)
                    if not (u.among_first(4)):
                        sp.wait_ge(s_pv, at(4 * u.n - 12))
                    for hh in range(HEADS):
                        for g4 in range(4):
                            sp.dma_start(vs[HT * g4:HT * g4 + HT, u.r, hh, :],
                                         xv[HT * hh:HT * hh + HT, 4 * g4:4 * g4 + 4, :].rearrange("p g w -> p (g w)")).then_inc(s_vs[u.r], 16)

            load_t(Unit(0, 0))
            run(sp, iteration)
            sp.wait_ge(s_pv, 4 * UNITS)
            for e in range(NE):
                sp.dma_start(w1[:, e * ET * FF:(e + 1) * ET * FF].rearrange("p (k f) -> p k f", k=ET), a["w1"][e]).then_inc(s_w1, 16)
            sp.dma_start(b1[:].rearrange("p (e c) -> p e c", e=NE), a["b1"]).then_inc(s_b, 16)
            sp.wait_ge(s_ph, UNITS)
            sp.dma_start(b2[:], a["b2"].partition_broadcast(P)).then_inc(s_b, 16)
            for e in range(NE):
                sp.dma_start(w2[:, e], a["w2"][e].rearrange("c p n -> p c n")).then_inc(s_w2, 16)

            def fetch(t):
                if not t.real():
                    return
                if not t.among_first(4):
                    sp.wait_ge(s_fs, at(16 * t.n - 48))
                row = sp.value_load(table[0:1, 0, bass.ds(at(t.n), 1)], min_val=0, max_val=NE * REGION)
                sp.dma_start(xg[:, t.r, :], sorted_x[bass.ds(row, P), :]).then_inc(s_fx[t.r], 16)

            sp.wait_ge(s_tab, 1)
            for g in range(2):
                sp.wait_ge(s_sc[g], 32 * UNITS // 2)
            sp.wait_ge(s_padd, 16 * (NE + 1))
            fetch(Unit(0, 0, TILES))
            run_tiles(sp, lambda t: fetch(t.plus(2)))

            def last(u):
                if u.real():
                    if not u.among_first(4):
                        sp.wait_ge(s_ln, at(4 * u.n - 15))
                    sp.dma_start(res[:, u.r], results[0:2 * T].rearrange("(u t c) e -> u t (c e)", t=P, c=2)[bass.ds(at(u.n), 1)]
                                 .rearrange("o t e -> (o t) e")).then_inc(s_rl[u.r], 16)
                    sp.dma_start(x2in[:, u.r], x2_dram[bass.ds(at(u.n), 1)].rearrange("o t e -> (o t) e")).then_inc(s_rl[u.r], 16)

            sp.wait_ge(s_fs, 16 * TILES)
            for g in range(2):
                sp.wait_ge(s_x2d[g], 16 * UNITS // 2)
            run_last(sp, last)

        @block.gpsimd
        def _(pool):
            for t, v in ((identf, 0.0), (identb, 0.0), (before, 1.0), (onesb, 1.0), (half, -0.5)):
                pool.memset(t[:], v).then_inc(s_k, 1)
            pool.memset(xv[:, :, 3 * D:3 * D + 1], 1.0).then_inc(s_k, 1)
            pool.memset(xv[:, :, 3 * D + 1:VW], 0.0).then_inc(s_k, 1)
            pool.memset(pad[:], 0.0).then_inc(s_k, 1)
            pool.iota(starts[:], [[REGION, NE]], base=0, channel_multiplier=0, allow_small_or_imprecise_dtypes=True)
            pool.iota(iotap[:], [[DUMP, 2]], base=0, channel_multiplier=1, allow_small_or_imprecise_dtypes=True)
            pool.iota(tiles[:], [[1, TILES]], base=0, channel_multiplier=0, allow_small_or_imprecise_dtypes=True)
            pool.iota(iota8[:], [[1, NE]], base=0, channel_multiplier=0, allow_small_or_imprecise_dtypes=True)
            pool.iota(cnt[:], [[REGION, NE]], base=0, channel_multiplier=0, allow_small_or_imprecise_dtypes=True)
            pool.iota(ids[:], [[1, 2]], base=0, channel_multiplier=2, allow_small_or_imprecise_dtypes=True).then_inc(s_k, 1)
            pool.wait_ge(s_k, NCONST - 3)
            for t in (identf, identb):
                pool.affine_select(out=t[:], in_=t[:], compare_op=ALU.not_equal, fill=1.0, base=0,
                                   pattern=[[-1, P]], channel_multiplier=1).then_inc(s_k, 1)
            pool.affine_select(out=before[:], in_=before[:], compare_op=ALU.is_ge, fill=0.0, base=-1,
                               pattern=[[1, P]], channel_multiplier=-1).then_inc(s_k, 1)
            pool.wait_ge(s_w, NLOADS)
            pool.wait_ge(s_k, NCONST)

            def rstd(which, ready, count, done):
                pool.wait_ge(ready, at(count))
                pool.tensor_tensor(rs[:, which:which + 1], ve[:, which:which + 1], half[:], ALU.pow).then_inc(done, 1)

            def iteration(st_, _):
                soft, attn, route, place = st_["soft"], st_["attn"], st_["route"], st_["place"]
                if route.real():
                    rstd(2, s_l5, 5 * route.n + 5, s_rs5)
                for k in range(16):
                    if soft.real():
                        hh, j = divmod(k, NJ)
                        c0 = (hh * NJ + j) * S
                        pool.wait_ge(s_exp, at(16 * soft.n + k + 1))
                        pool.tensor_tensor(low[:, c0:c0 + S], prob[:, c0:c0 + S], prob_hi[:, 2 * c0 + 1:2 * c0 + 2 * S:2],
                                           ALU.subtract).then_inc(s_lo, 1)
                    if k == 4 and attn.real():
                        pool.wait_ge(s_xp[attn.r], at(32 * attn.b + 32))
                        if not attn.first():
                            pool.wait_ge(s_x1, at(attn.n))
                        pool.tensor_tensor(xb[:, 0, :], xin[:, attn.r, :], bo[:], ALU.add).then_inc(s_xb, 1)
                        pool.tensor_tensor(xb[:, 1, :], xin[:, attn.r, :], beta[:], ALU.add).then_inc(s_xb, 1)
                    if k == 7 and place.real():
                        pool.wait_ge(s_rd, at(7 * place.n + 7))
                        pool.wait_ge(s_pl2, at(place.n + 1))
                        g = place.r % 2
                        pool.nop(nofuse=True)
                        for c in range(2):
                            pool.indirect_dma_start(sorted_x, bass.IndirectOffsetOnAxis(ap=slot[:, g, c:c + 1], axis=0),
                                                    pl[:, g, c, :], None, bounds_check=NE * REGION + P - 1).then_inc(s_sc[g], 16)
                    if k == 14 and attn.real():
                        rstd(0, s_l1, 4 * attn.n + 4, s_rs1)
                    if k == 15 and attn.real():
                        rstd(1, s_l2, 6 * attn.n + 6, s_rs2)

            run(pool, iteration)
            pool.wait_ge(s_pad, 3)
            for e in range(NE):
                pool.indirect_dma_start(sorted_x, bass.IndirectOffsetOnAxis(ap=padto[:, e:e + 1], axis=0),
                                        pad[:], None, bounds_check=NE * REGION + P - 1).then_inc(s_padd, 16)
            pool.dma_start(sorted_x[NE * REGION:NE * REGION + P, :], pad[:]).then_inc(s_padd, 16)

            def scatter(t):
                t = t.plus(-1)
                if t.real():
                    pool.wait_ge(s_fo, at(t.n + 1))
                    if not t.first():
                        pool.wait_ge(s_fs, at(16 * t.n))
                    pool.nop(nofuse=True)
                    pool.indirect_dma_start(results, bass.IndirectOffsetOnAxis(ap=xg[:, t.r, E + 1:E + 2].bitcast(U32), axis=0),
                                            yo[:, t.r % 2, :], None, bounds_check=2 * T + P - 1).then_inc(s_fs, 16)

            run_tiles(pool, scatter)

            def last(u):
                if u.real():
                    pool.wait_ge(s_rl[u.r], at(32 * u.b + 32))
                    pool.tensor_tensor(tot[:, u.r, :], res[:, u.r, 0:E], res[:, u.r, E:2 * E], ALU.add).then_inc(s_ra, 1)
                u = u.plus(-1)
                if u.real():
                    pool.wait_ge(s_ln, at(4 * u.n + 4))
                    pool.tensor_tensor(frs[:, u.r:u.r + 1], fve[:, u.r:u.r + 1], half[:], ALU.pow).then_inc(s_lr, 1)

            run_last(pool, last)

        @block.tensor
        def _(pe):
            pe.wait_ge(s_w, NLOADS)
            pe.wait_ge(s_k, NCONST)
            read = {}

            def bank(z, reader, count):
                if z in read:
                    pe.wait_ge(read[z][0], at(read[z][1]))
                read[z] = (reader, count)

            def side(k, st_):
                front, peak, row, attn = st_["front"], st_["peak"], st_["row"], st_["attn"]
                cross, route, place = st_["cross"], st_["route"], st_["place"]
                if k == 0 and row.real():
                    pe.wait_ge(s_xm, at(4 * row.n + 4))
                    bank(1, s_mrow, row.n + 1)
                    pe.nop(nofuse=True)
                    nc.tensor.transpose(zb(1)[0:48, 0:P], xm[:].rearrange("p a b -> p (a b)"), identb[:]).then_inc(s_mt, 1)
                if k == 0 and front.real():
                    pe.wait_ge(s_xt[front.r], at(32 * front.b + 32))
                    bank(0, s_q32, 2 * front.n + 1)
                    for e in range(ET):
                        last = nc.tensor.matmul(pz[:, 0, :], xt[:, front.r, e, :], wqkv[:, e, 0:2 * E], start=e == 0, stop=e == ET - 1)
                    last.then_inc(s_pqk, 1)
                if k == 1 and front.real():
                    bank(1, s_q32, 2 * front.n + 2)
                    for e in range(ET):
                        last = nc.tensor.matmul(pz[:, 1, 0:E], xt[:, front.r, e, :], wqkv[:, e, 2 * E:3 * E], start=e == 0, stop=e == ET - 1)
                    last.then_inc(s_pvv, 1)
                if k == 2 and cross.real():
                    pe.wait_ge(s_x1, at(cross.n + 1))
                    bank(0, s_x1te, cross.n + 1)
                    for e in range(ET):
                        last = nc.tensor.transpose(pz[:, 0, e * P:e * P + P], x1[:, cross.r % 2, e * P:e * P + P], identf[:])
                    last.then_inc(s_x1t, 1)
                if k == 3 and route.real():
                    pe.wait_ge(s_x2, at(route.n + 1))
                    bank(1, s_x2te, route.n + 1)
                    for e in range(ET):
                        last = nc.tensor.transpose(pz[:, 1, e * P:e * P + P], pl[:, route.r % 2, 0, e * P:e * P + P], identf[:])
                    last.then_inc(s_x2t, 1)
                if k == 4 and cross.real():
                    bank(0, s_qte, cross.n + 1)
                    for m in range(ET):
                        for e in range(ET):
                            last = nc.tensor.matmul(pz[:, 0, m * P:m * P + P], wqx[:, e, m * P:m * P + P], x1t[:, e, :], start=e == 0, stop=e == ET - 1)
                    last.then_inc(s_qt, 1)
                if k == 4 and place.real():
                    pe.wait_ge(s_rc, at(8 * place.n + 8))
                    bank(1, s_rd, 7 * place.n + 5)
                    nc.tensor.matmul(pz[:, 1, 0:NE], before[:], chosen[:], start=True, stop=True)
                    nc.tensor.matmul(pz[:, 1, NE:2 * NE], onesb[:], chosen[:], start=True, stop=True).then_inc(s_pf, 1)
                if k == 5 and peak.real():
                    bank(1, s_kte, peak.n + 1)
                    for m in range(ET):
                        for e in range(ET):
                            last = nc.tensor.matmul(pz[:, 1, m * P:m * P + P], wkx[:, e, m * P:m * P + P], ct[:, peak.r, e, :], start=e == 0, stop=e == ET - 1)
                    last.then_inc(s_kt, 1)
                if 6 <= k < 10 and front.real():
                    if k == 6:
                        pe.wait_ge(s_rep, at(front.n + 1))
                    src = xq if k < 8 else xk
                    z = k % 2
                    bank(z, s_stk, 4 * front.n + k - 5)
                    for t in range(8):
                        g = 8 * (k % 2) + t
                        group = 4 * (g % 4) + g // 4
                        last = nc.tensor.transpose(zb(z)[0:KROWS, t * P:t * P + P], src[:, group].rearrange("p a d -> p (a d)"), identb[:])
                    last.then_inc(s_tr, 1)
                if k == 10 and cross.real():
                    pe.wait_ge(s_kte, at(4 * cross.b + 4))
                    bank(0, s_t, 2 * cross.n + 1)
                    par = at(cross.b) % 2
                    for e in range(ET):
                        last = nc.tensor.matmul(pz[:, 0, :], qxt[:, e, :], kx[:, bass.ds(par * (ET * S) + e * S, S)], start=e == 0, stop=e == ET - 1)
                    last.then_inc(s_s, 1)
                if k == 11 and attn.real():
                    pe.wait_ge(s_c, at(2 * attn.n + 2))
                    bank(1, s_ct, attn.n + 1)
                    pe.nop(nofuse=True)
                    for hh in range(HEADS):
                        last = nc.tensor.transpose(pz[0:64, 1, hh * P:hh * P + P], cx[:, hh * 64:hh * 64 + 64], identf[:])
                    last.then_inc(s_ctr, 1)
                if k == 12 and route.real():
                    pe.wait_ge(s_x2te, at(route.n + 1))
                    bank(0, s_rc, 8 * route.n + 1)
                    for e in range(ET):
                        last = nc.tensor.matmul(pz[:, 0, 0:NE], x2t[:, e, :], rw[:, e, :], start=e == 0, stop=e == ET - 1)
                    last.then_inc(s_rt, 1)
                if k == 13 and attn.real():
                    bank(1, s_l1, 4 * attn.n + 1)
                    for e in range(ET):
                        last = nc.tensor.matmul(pz[:, 1, 0:E], cxt[:, e, :], wo[:, e, :], start=e == 0, stop=e == ET - 1)
                    last.then_inc(s_o, 1)
                if k == 14 and cross.real():
                    pe.wait_ge(s_e5, at(cross.n + 1))
                    bank(0, s_pte, cross.n + 1)
                    for j in range(QB):
                        last = nc.tensor.transpose(pz[:, 0, j * P:j * P + P], p5[:, j * P:j * P + P], identf[:])
                    last.then_inc(s_pt, 1)
                if k == 15 and peak.real():
                    bank(1, s_vte, peak.n + 1)
                    for e in range(ET):
                        last = nc.tensor.matmul(pz[:, 1, 0:E], ct[:, peak.r, e, :], wvx[:, e, :], start=e == 0, stop=e == ET - 1)
                    last.then_inc(s_vt, 1)
                if k == 15 and cross.real():
                    pe.wait_ge(s_vte, at(4 * cross.b + 4))
                    bank(0, s_l5, 5 * cross.n + 2)
                    par = at(cross.b) % 2
                    for j in range(QB):
                        last = nc.tensor.matmul(pz[:, 0, 0:E], p5t[:, j, :], vx[:, bass.ds(par * (QB * E) + j * E, E)], start=j == 0, stop=j == QB - 1)
                    last.then_inc(s_pv5, 1)

            def iteration(st_, entry):
                peak, soft = st_["peak"], st_["soft"]
                if entry:
                    read[0] = (s_l5, 5 * st_["cross"].plus(-1).n + 2)
                    read[1] = (s_vte, st_["peak"].plus(-1).n + 1)
                for k in range(16):
                    hh, j = divmod(k, NJ)
                    q0 = hh * S
                    if peak.real():
                        if k == 0:
                            pe.wait_ge(s_stk, at(4 * peak.n + 4))
                        if not (peak.first() and k < 2):
                            pe.wait_ge(s_red, at(16 * peak.n + k - 1))
                        nc.tensor.matmul(pm[:, k % 2, :], qs[peak.r][0:KROWS, q0 + j * P:q0 + j * P + P],
                                         ks[peak.r][0:KROWS, q0:q0 + S], start=True, stop=True).then_inc(s_mxq, 1)
                    if soft.real():
                        if k == 0:
                            pe.wait_ge(s_mr[soft.r], at(48 * soft.b + 48))
                        if not (soft.first() and k < 2):
                            pe.wait_ge(s_exp, at(16 * soft.n + k - 1))
                        nc.tensor.matmul(pe_[:, k % 2, :], ks[soft.r][0:KROWS + 3, q0 + j * P:q0 + j * P + P],
                                         qs[soft.r][0:KROWS + 3, q0:q0 + S], start=True, stop=True).then_inc(s_qkt, 1)
                    u = soft if k >= 6 else st_["attn"]
                    if u.real():
                        hv, c = divmod((k - 6) % 16, NJ)
                        if c == 0:
                            pe.wait_ge(s_lo, at(16 * u.n + 4 * hv + 4))
                            if hv == 0:
                                pe.wait_ge(s_vs[u.r], at(256 * u.b + 256))
                            if hv % 2 == 0 and not u.first():
                                pe.wait_ge(s_vsum, at(2 * u.n + hv // 2 - 1))
                        dst = pv[:, hv // 2, (hv % 2) * NJ * VW + c * VW:(hv % 2) * NJ * VW + c * VW + 3 * D + 1]
                        for jj in range(NJ):
                            p0 = (hv * NJ + jj) * S + c * P
                            v = vs[:, u.r, hv, jj * VW:jj * VW + 3 * D + 1]
                            nc.tensor.matmul(dst, prob_hi[:, 2 * p0 + 1:2 * p0 + 2 * P:2], v, start=jj == 0, stop=False)
                            last = nc.tensor.matmul(dst, low[:, p0:p0 + P], v, start=False, stop=jj == NJ - 1)
                        if c == NJ - 1:
                            last.then_inc(s_pv, 1)
                    side(k, st_)

            run(pe, iteration)

            pe.wait_ge(s_w2, 16 * NE)
            pe.wait_ge(s_tab, 1)

            def tile(t):
                n = t.plus(1)
                if n.real():
                    pe.wait_ge(s_fx[n.r], at(16 * n.b + 16))
                    if not n.among_first(2):
                        pe.wait_ge(s_fxt, at(n.n - 1))
                    for e in range(ET):
                        last = nc.tensor.transpose(pz[:, n.r % 2, e * P:e * P + P], xg[:, n.r, e * P:e * P + P], identf[:])
                    last.then_inc(s_ft, 1)
                if t.real():
                    hbank = (pm, pe_)[t.r % 2]
                    xT = xgt[t.r % 2]
                    pe.wait_ge(s_fxt, at(t.n + 1))
                    pe.wait_ge(s_fw, at(t.n + 1))
                    for c in range(FC):
                        if c % 4 == 0 and not t.among_first(2):
                            pe.wait_ge(s_fg, at(2 * t.n - 3 + c // 4))
                        for e in range(ET):
                            last = nc.tensor.matmul(hbank[:, c // 4, (c % 4) * P:(c % 4) * P + P],
                                                    w1f[:, t.r % 2, e * FF + c * P:e * FF + c * P + P], xT[:, e, :],
                                                    start=e == 0, stop=e == ET - 1)
                        if c % 4 == 3:
                            last.then_inc(s_fh, 1)
                o = t.plus(-1)
                if o.real():
                    expert = pe.value_load(table[0:1, 1, bass.ds(at(o.n), 1)], min_val=0, max_val=NE - 1)
                    if not o.among_first(2):
                        pe.wait_ge(s_fo, at(o.n - 1))
                    for c in range(FC):
                        if c % 4 == 0:
                            pe.wait_ge(s_fg, at(2 * o.n + 1 + c // 4))
                        last = nc.tensor.matmul(pv[:, o.r % 2, 0:E], hidden[o.r % 2][:, c * P:c * P + P],
                                                arena2[:, bass.ds(expert * (FC * E) + c * E, E)], start=c == 0, stop=c == FC - 1)
                    last.then_inc(s_fy, 1)

            run_tiles(pe, tile)

        @block.scalar
        def _(act):
            act.wait_ge(s_w, NLOADS)
            act.wait_ge(s_k, NCONST)
            act.wait_ge(s_c2, 2)

            def stack_evac(n, front, z):
                dst = (qs if n < 2 else ks)[front.r]
                h = n % 2
                act.wait_ge(s_tr, at(4 * front.n + n + 1))
                o = dst[0:KROWS, :].rearrange("p (h g s) -> p g h s", h=HEADS, g=G)[:, 8 * h:8 * h + 8]
                act.activation(o, zb(z)[0:KROWS, :].rearrange("p (g h s) -> p g h s", g=8, h=HEADS), ACT.Copy).then_inc(s_stk, 1)

            def side(k, st_):
                front, peak, row, attn = st_["front"], st_["peak"], st_["row"], st_["attn"]
                cross, route = st_["cross"], st_["route"]
                if k == 1 and row.real():
                    act.wait_ge(s_mt, at(row.n + 1))
                    if not row.first():
                        act.wait_ge(s_mr[row.plus(-1).r], at(48 * row.plus(-1).b + 48))
                    act.activation(mrow[0:48, :], zb(1)[0:48, 0:P], ACT.Copy).then_inc(s_mrow, 1)
                if k == 1 and route.real():
                    act.wait_ge(s_x2, at(route.n + 1))
                    act.activation(pl[:, route.r % 2, 1, 0:E], pl[:, route.r % 2, 0, 0:E], ACT.Copy).then_inc(s_pl2, 1)
                if k == 2 and front.real():
                    act.wait_ge(s_q32, at(2 * front.n + 2))
                    if not front.first():
                        before_ = front.plus(-1)
                        act.wait_ge(s_tr, at(4 * front.n))
                        act.wait_ge(s_vs[before_.r], at(256 * before_.b + 256))
                    act.activation(xq[:, :, 0, :], q32[:, 0:E].rearrange("p (g d) -> p g d", g=G), ACT.Copy)
                    act.activation(xk[:, :, 0, :], q32[:, E:2 * E].rearrange("p (g d) -> p g d", g=G), ACT.Copy)
                    act.activation(xv[:, :, 0:D], q32[:, 2 * E:3 * E].rearrange("p (g d) -> p g d", g=G), ACT.Copy).then_inc(s_h, 1)
                if k == 3 and cross.real():
                    act.wait_ge(s_x1t, at(cross.n + 1))
                    if not cross.first():
                        act.wait_ge(s_qt, at(cross.n))
                    act.activation(x1t[:], pz[:, 0, 0:E].rearrange("p (e t) -> p e t", e=ET), ACT.Copy).then_inc(s_x1te, 1)
                if k == 4 and front.real():
                    act.wait_ge(s_r, at(front.n + 1))
                    act.activation(xq[:, :, 3, :], q32[:, 0:E].rearrange("p (g d) -> p g d", g=G), ACT.Copy)
                    act.activation(xk[:, :, 1, :], q32[:, E:2 * E].rearrange("p (g d) -> p g d", g=G), ACT.Copy)
                    act.activation(xv[:, :, D:2 * D], q32[:, 2 * E:3 * E].rearrange("p (g d) -> p g d", g=G), ACT.Copy).then_inc(s_m, 1)
                if k == 4 and route.real():
                    act.wait_ge(s_x2t, at(route.n + 1))
                    if not route.first():
                        act.wait_ge(s_rt, at(route.n))
                    act.activation(x2t[:], pz[:, 1, 0:E].rearrange("p (e t) -> p e t", e=ET), ACT.Copy).then_inc(s_x2te, 1)
                if k == 5 and cross.real():
                    act.wait_ge(s_qt, at(cross.n + 1))
                    if not cross.first():
                        act.wait_ge(s_s, at(cross.n))
                    for m in range(ET):
                        last = act.activation(qxt[:, m, :], pz[:, 0, m * P:m * P + P], ACT.Identity, bias=bqx[:, m:m + 1])
                    last.then_inc(s_qte, 1)
                if k == 6 and peak.real():
                    act.wait_ge(s_kt, at(peak.n + 1))
                    if not peak.among_first(8) and peak.r == 0:
                        act.wait_ge(s_s, at(4 * peak.b - 4))
                    par = at(peak.b) % 2
                    for m in range(ET):
                        last = act.activation(kx[:, bass.ds(par * (ET * S) + m * S + peak.r * P, P)], pz[:, 1, m * P:m * P + P],
                                              ACT.Identity, bias=bkx[:, m:m + 1])
                    last.then_inc(s_kte, 1)
                if 7 <= k < 11 and front.real():
                    stack_evac(k - 7, front, (k - 7) % 2)
                if k == 8 and cross.real():
                    act.wait_ge(s_xp[cross.r], at(32 * cross.b + 32))
                    if not cross.first():
                        act.wait_ge(s_t, at(2 * cross.n - 1))
                    act.activation(phs[:], phi[:, cross.r, :], ACT.Copy, scale=coef[:, 1:2]).then_inc(s_ph, 1)
                if k == 11 and cross.real():
                    act.wait_ge(s_t, at(2 * cross.n + 2))
                    if not cross.first():
                        act.wait_ge(s_pt, at(cross.n))
                        act.wait_ge(s_l5, at(5 * cross.n - 3))
                    act.activation(p5[:], att[:], ACT.Exp, bias=nmx5[:, 1:2], scale=1.0 / 16, accum_out=sum5[:, 0:1]).then_inc(s_e5, 1)
                if k == 12 and attn.real():
                    act.wait_ge(s_ctr, at(attn.n + 1))
                    if not attn.first():
                        act.wait_ge(s_o, at(attn.n))
                    v = pz[0:64, 1, :].rearrange("p (h e a s) -> p a e h s", h=HEADS, e=ET, a=2)
                    for par in range(2):
                        last = act.activation(cxt[64 * par:64 * par + 64].rearrange("p e (h s) -> p e h s", h=HEADS), v[:, par], ACT.Copy)
                    last.then_inc(s_ct, 1)
                if k == 14 and route.real():
                    act.wait_ge(s_rc, at(8 * route.n + 4))
                    act.activation(gate[:, 1:2], gate[:, 0:1], ACT.Exp).then_inc(s_e2, 1)
                if k == 15 and cross.real():
                    act.wait_ge(s_pt, at(cross.n + 1))
                    if not cross.first():
                        act.wait_ge(s_pv5, at(cross.n))
                    act.activation(p5t[:], pz[:, 0, :].rearrange("p (j t) -> p j t", j=QB), ACT.Copy).then_inc(s_pte, 1)

            def iteration(st_, _):
                soft = st_["soft"]
                for k in range(16):
                    if soft.real():
                        hh, j = divmod(k, NJ)
                        c0 = (hh * NJ + j) * S
                        if j == 0 and not soft.first():
                            act.wait_ge(s_pv, at(4 * soft.n - 3 + hh))
                        act.wait_ge(s_qkt, at(16 * soft.n + k + 1))
                        act.activation(prob[:, c0:c0 + S], pe_[:, k % 2, :], ACT.Exp, scale=0.25).then_inc(s_exp, 1)
                    side(k, st_)

            run(act, iteration)

            act.wait_ge(s_tab, 1)
            act.wait_ge(s_b, 32)

            def tile(t):
                if not t.real():
                    return
                expert = act.value_load(table[0:1, 1, bass.ds(at(t.n), 1)], min_val=0, max_val=NE - 1)
                if not t.among_first(2):
                    act.wait_ge(s_fy, at(t.n - 1))
                for c in range(FC):
                    if c % 4 == 0:
                        act.wait_ge(s_fh, at(2 * t.n + 1 + c // 4))
                    last = act.activation(hidden[t.r % 2][:, c * P:c * P + P], (pm, pe_)[t.r % 2][:, c // 4, (c % 4) * P:(c % 4) * P + P],
                                          ACT.Gelu, bias=b1[:, bass.ds(expert * FC + c, 1)])
                    if c % 4 == 3:
                        last.then_inc(s_fg, 1)

            run_tiles(act, tile)

            def last(u):
                u = u.plus(-1)
                if u.real():
                    act.wait_ge(s_ly, at(u.n + 1))
                    act.dma_start(out[bass.ds(at(u.n), 1)].rearrange("o t e -> (o t) e"), fout[:, u.r]).then_inc(s_lo_[u.r], 16)

            run_last(act, last)
            for g in range(4):
                act.wait_ge(s_lo_[g], 16 * UNITS // 4)

        @block.vector
        def _(dve):
            for g in range(4):
                dve.memset(ks[g][KROWS:KROWS + 3, :], 1.0).then_inc(s_k, 1)
            dve.wait_ge(s_w, NLOADS)
            dve.wait_ge(s_k, NCONST)
            dve.tensor_tensor(coef[:, 0:1], betas[:, 0:1], betas[:, 1:2], ALU.add).then_inc(s_c2, 1)
            dve.wait_ge(s_c2, 1)
            dve.tensor_scalar(coef[:, 1:2], coef[:, 0:1], betas[:, 2:3], 16.0, ALU.subtract, ALU.mult).then_inc(s_c2, 1)

            def groups(t):
                return t.rearrange("p (g d) -> p g d", g=G)

            def stats(src, w, s, n0):
                dve.wait_ge(s, at(n0))
                dve.bn_stats(st[:, w, :], src).then_inc(s, 1)
                dve.wait_ge(s, at(n0 + 1))
                dve.nop(nofuse=True)
                dve.bn_aggr(mv[:, w, :], st[:, w, :]).then_inc(s, 1)
                dve.wait_ge(s, at(n0 + 2))
                dve.tensor_scalar(ve[:, w:w + 1], mv[:, w, 1:2], EPS, None, ALU.add).then_inc(s, 1)

            def average(q, u):
                dve.wait_ge(s_pv, at(4 * u.n + 2 * q + 2))
                v = pv[:, q, 0:8 * VW].rearrange("p (a w) -> p a w", w=VW)
                dve.tensor_reduce(psums[:], v[:, :, 0:3 * D].rearrange("p a (t d) -> p a d t", t=3), AX.X, ALU.add)
                dve.reciprocal(prec[:], v[:, :, 3 * D]).then_inc(s_vsum, 1)
                dve.wait_ge(s_vsum, at(2 * u.n + q + 1))
                if q == 0 and not u.first():
                    dve.wait_ge(s_ctr, at(u.n))
                dve.tensor_tensor(cx[:, q * P:q * P + P].rearrange("p (a d) -> p a d", d=D), psums[:],
                                  prec[:].unsqueeze(2).to_broadcast([P, 8, D]), ALU.mult).then_inc(s_c, 1)

            def side(k, st_):
                front, peak, soft, attn = st_["front"], st_["peak"], st_["soft"], st_["attn"]
                cross, route, place = st_["cross"], st_["route"], st_["place"]
                if k == 0 and route.real():
                    g = route.r % 2
                    dve.wait_ge(s_rs5, at(route.n + 1))
                    if not (route.among_first(2)):
                        old = route.plus(-2)
                        uses = 2 * old.b + old.r // 2
                        dve.wait_ge(s_x2d[g], at(16 * uses + 16))
                        dve.wait_ge(s_sc[g], at(32 * uses + 32))
                    dve.tensor_scalar(pl[:, g, 0, 0:E], y2[:], mv[:, 2, 0:1], rs[:, 2:3], ALU.subtract, ALU.mult).then_inc(s_x2, 1)
                if k == 1 and front.real():
                    dve.wait_ge(s_pqk, at(front.n + 1))
                    dve.tensor_tensor(q32[:, 0:2 * E], pz[:, 0, :], bqkv[:, 0:2 * E], ALU.add).then_inc(s_q32, 1)
                if k == 1 and front.real():
                    dve.wait_ge(s_pvv, at(front.n + 1))
                    dve.tensor_tensor(q32[:, 2 * E:3 * E], pz[:, 1, 0:E], bqkv[:, 2 * E:3 * E], ALU.add).then_inc(s_q32, 1)
                if k == 3 and front.real():
                    dve.wait_ge(s_h, at(front.n + 1))
                    for t, h in ((0, xq[:, :, 0, :]), (1, xk[:, :, 0, :]), (2, xv[:, :, 0:D])):
                        q = groups(q32[:, t * E:t * E + E])
                        last = dve.tensor_tensor(q, q, h, ALU.subtract)
                    last.then_inc(s_r, 1)
                if k == 5 and place.real():
                    g = place.r % 2
                    c0 = 7 * place.n
                    dve.wait_ge(s_e2, at(place.n + 1))
                    dve.tensor_scalar(gate[:, 2:3], gate[:, 1:2], 1.0, None, ALU.add).then_inc(s_rd, 1)
                    dve.wait_ge(s_pf, at(place.n + 1))
                    dve.tensor_tensor(base[:], pz[:, 1, 0:NE], cnt[:], ALU.add).then_inc(s_rd, 1)
                    dve.wait_ge(s_rd, at(c0 + 2))
                    dve.reciprocal(pl[:, g, 0, E:E + 1], gate[:, 2:3]).then_inc(s_rd, 1)
                    for c in range(2):
                        last = dve.tensor_tensor_reduce(out=ohb[:, c, :], in0=oh[:, c, :], in1=base[:], scale=1.0, scalar=0.0,
                                                        op0=ALU.mult, op1=ALU.add, accum_out=slotf[:, c:c + 1])
                    last.then_inc(s_rd, 1)
                    dve.tensor_tensor(cnt[:], cnt[:], pz[:, 1, NE:2 * NE], ALU.add).then_inc(s_rd, 1)
                    dve.wait_ge(s_rd, at(c0 + 5))
                    dve.tensor_copy(slot[:, g, :], slotf[:])
                    dve.tensor_tensor(pl[:, g, 1, E:E + 1], gate[:, 1:2], pl[:, g, 0, E:E + 1], ALU.mult).then_inc(s_rd, 1)
                    dve.tensor_copy(pl[:, g, :, E + 1].bitcast(I32), ids[:]).then_inc(s_rd, 1)
                    dve.tensor_scalar(ids[:], ids[:], 2.0 * P, None, ALU.add)
                if k == 5 and front.real():
                    dve.wait_ge(s_m, at(front.n + 1))
                    dve.tensor_tensor(xv[:, :, 2 * D:3 * D], groups(q32[:, 2 * E:3 * E]), xv[:, :, D:2 * D], ALU.subtract).then_inc(s_xv, 1)
                    dve.tensor_tensor(xq[:, :, 5, :], groups(q32[:, 0:E]), xq[:, :, 3, :], ALU.subtract)
                    dve.tensor_tensor(xk[:, :, 2, :], groups(q32[:, E:2 * E]), xk[:, :, 1, :], ALU.subtract)
                    dve.tensor_copy(xq[:, :, 1:3, :], xq[:, :, 0:1, :].to_broadcast([P, G, 2, D]))
                    dve.tensor_copy(xq[:, :, 4, :], xq[:, :, 3, :])
                    dve.tensor_copy(xk[:, :, 3:5, :], xk[:, :, 0:2, :])
                    dve.tensor_copy(xk[:, :, 5, :], xk[:, :, 0, :]).then_inc(s_rep, 1)
                if k == 6 and attn.real():
                    average(1, attn)
                if k == 10 and cross.real():
                    dve.wait_ge(s_s, at(cross.n + 1))
                    dve.wait_ge(s_ph, at(cross.n + 1))
                    if not cross.first():
                        dve.wait_ge(s_e5, at(cross.n))
                    dve.nop(nofuse=True)
                    dve.tensor_tensor_reduce(out=att[:], in0=pz[:, 0, :], in1=phs[:], scale=1.0, scalar=-3.0e38,
                                             op0=ALU.add, op1=ALU.max, accum_out=nmx5[:, 0:1]).then_inc(s_t, 1)
                    dve.wait_ge(s_t, at(2 * cross.n + 1))
                    dve.tensor_scalar(nmx5[:, 1:2], nmx5[:, 0:1], -1.0 / 16, None, ALU.mult).then_inc(s_t, 1)
                if k == 12 and route.real():
                    c0 = 8 * route.n
                    dve.wait_ge(s_rt, at(route.n + 1))
                    dve.tensor_copy(lg[:], pz[:, 0, 0:NE]).then_inc(s_rc, 1)
                    dve.wait_ge(s_rc, at(c0 + 1))
                    dve.nop(nofuse=True)
                    dve.max(top[:], lg[:]).then_inc(s_rc, 1)
                    dve.wait_ge(s_rc, at(c0 + 2))
                    dve.nop(nofuse=True)
                    dve.max_index(topi[:], top[:], lg[:]).then_inc(s_rc, 1)
                    dve.tensor_tensor(gate[:, 0:1], top[:, 1:2], top[:, 0:1], ALU.subtract).then_inc(s_rc, 1)
                    dve.wait_ge(s_rc, at(c0 + 4))
                    dve.tensor_copy(topf[:], topi[:, 0:2]).then_inc(s_rc, 1)
                    dve.wait_ge(s_rc, at(c0 + 5))
                    for c in range(2):
                        dve.tensor_scalar(oh[:, c, :], iota8[:], topf[:, c:c + 1], None, ALU.is_equal).then_inc(s_rc, 1)
                    dve.wait_ge(s_rc, at(c0 + 7))
                    dve.tensor_tensor(chosen[:], oh[:, 0, :], oh[:, 1, :], ALU.add).then_inc(s_rc, 1)
                if k == 14 and soft.real():
                    average(0, soft)
                if k == 14 and attn.real():
                    dve.wait_ge(s_o, at(attn.n + 1))
                    dve.wait_ge(s_xb, at(2 * attn.n + 2))
                    dve.tensor_tensor(y1[:], pz[:, 1, 0:E], xb[:, 0, :], ALU.add).then_inc(s_l1, 1)
                    stats(y1[:], 0, s_l1, 4 * attn.n + 1)
                if k == 15 and attn.real():
                    c0 = 6 * attn.n
                    dve.wait_ge(s_rs1, at(attn.n + 1))
                    dve.tensor_scalar(z1[:], y1[:], mv[:, 0, 0:1], rs[:, 0:1], ALU.subtract, ALU.mult).then_inc(s_l2, 1)
                    dve.wait_ge(s_l2, at(c0 + 1))
                    dve.tensor_tensor(z1[:], z1[:], gamma[:], ALU.mult).then_inc(s_l2, 1)
                    dve.wait_ge(s_l2, at(c0 + 2))
                    dve.tensor_tensor(z1[:], z1[:], xb[:, 1, :], ALU.add).then_inc(s_l2, 1)
                    stats(z1[:], 1, s_l2, c0 + 3)
                if k == 15 and peak.real():
                    dve.wait_ge(s_vt, at(peak.n + 1))
                    par = at(peak.b) % 2
                    dve.tensor_tensor(vx[:, bass.ds(par * (QB * E) + peak.r * E, E)], pz[:, 1, 0:E], bvx[:], ALU.add).then_inc(s_vte, 1)
                if k == 15 and cross.real():
                    dve.wait_ge(s_e5, at(cross.n + 1))
                    dve.reciprocal(sum5[:, 1:2], sum5[:, 0:1]).then_inc(s_l5, 1)
                if k == 15 and attn.real():
                    dve.wait_ge(s_rs2, at(attn.n + 1))
                    if not (attn.among_first(2)):
                        dve.wait_ge(s_x1t, at(attn.n - 1))
                    dve.tensor_scalar(x1[:, attn.r % 2, :], z1[:], mv[:, 1, 0:1], rs[:, 1:2], ALU.subtract, ALU.mult).then_inc(s_x1, 1)
                if k == 15 and cross.real():
                    dve.wait_ge(s_l5, at(5 * cross.n + 1))
                    dve.wait_ge(s_pv5, at(cross.n + 1))
                    dve.scalar_tensor_tensor(out=y2[:], in0=pz[:, 0, 0:E], scalar=sum5[:, 1:2], in1=x1[:, cross.r % 2, :],
                                             op0=ALU.mult, op1=ALU.add).then_inc(s_l5, 1)
                    stats(y2[:], 2, s_l5, 5 * cross.n + 2)

            def iteration(st_, _):
                row, peak = st_["row"], st_["peak"]
                if row.real():
                    c0 = 4 * row.n
                    m = nmx[:, row.r % 2, :]
                    dve.wait_ge(s_red, at(16 * row.n + 16))
                    if not row.first():
                        dve.wait_ge(s_mt, at(row.n))
                    dve.tensor_copy(xm[:, 0, :], m).then_inc(s_xm, 1)
                    dve.wait_ge(s_xm, at(c0 + 1))
                    dve.tensor_tensor(xmr[:, 0, :], m, xm[:, 0, :], ALU.subtract).then_inc(s_xm, 1)
                    dve.wait_ge(s_xm, at(c0 + 2))
                    dve.tensor_copy(xm[:, 1, :], xmr[:, 0, :]).then_inc(s_xm, 1)
                    dve.wait_ge(s_xm, at(c0 + 3))
                    dve.tensor_tensor(xm[:, 2, :], xmr[:, 0, :], xm[:, 1, :], ALU.subtract).then_inc(s_xm, 1)
                for k in range(16):
                    if peak.real():
                        dve.wait_ge(s_mxq, at(16 * peak.n + k + 1))
                        dve.tensor_reduce(nmx[:, peak.r % 2, k:k + 1], pm[:, k % 2, :], AX.X, ALU.max, negate=True).then_inc(s_red, 1)
                    side(k, st_)

            run(dve, iteration)

            dve.wait_ge(s_rd, 7 * UNITS)
            dve.tensor_copy(pad[:, E + 1:E + 2].bitcast(I32), iotap[:, 1:2]).then_inc(s_pad, 1)
            dve.tensor_scalar(padf[:], cnt[:], iotap[:, 0:1], None, ALU.add).then_inc(s_pad, 1)
            dve.wait_ge(s_pad, 2)
            dve.tensor_copy(padto[:], padf[:]).then_inc(s_pad, 1)

            def step(n):
                dve.wait_ge(s_plan, n)

            one = slice(0, 1)
            dve.tensor_tensor(plan[:, 0, :], cnt[one], starts[one], ALU.subtract).then_inc(s_plan, 1)
            step(1)
            dve.tensor_scalar(cnt_i[:, 0, :], plan[:, 0, :], float(P - 1), None, ALU.add).then_inc(s_plan, 1)
            step(2)
            dve.tensor_scalar(cnt_i[:, 1, :], cnt_i[:, 0, :], P.bit_length() - 1, None, ALU.logical_shift_right).then_inc(s_plan, 1)
            step(3)
            dve.tensor_copy(plan[:, 1, :], cnt_i[:, 1, :]).then_inc(s_plan, 1)
            step(4)
            dve.tensor_scalar(plan[:, 3, :], plan[:, 1, :], -float(P), float(REGION), ALU.mult, ALU.add).then_inc(s_plan, 1)
            dve.tensor_copy(plan[:, 2, 0:1], plan[:, 1, 0:1]).then_inc(s_plan, 1)
            for e in range(1, NE):
                step(5 + e)
                dve.tensor_tensor(plan[:, 2, e:e + 1], plan[:, 2, e - 1:e], plan[:, 1, e:e + 1], ALU.add).then_inc(s_plan, 1)
            n0 = 5 + NE
            step(n0)
            tb = tiles[:].unsqueeze(2).to_broadcast([1, TILES, NE])
            dve.tensor_tensor(past[:], tb, plan[:, 2:3, :].to_broadcast([1, TILES, NE]), ALU.is_ge).then_inc(s_plan, 1)
            step(n0 + 1)
            dve.tensor_tensor(jump[:], past[:], plan[:, 3:4, :].to_broadcast([1, TILES, NE]), ALU.mult).then_inc(s_plan, 1)
            dve.tensor_reduce(tabf[:, 0, :], past[:], AX.X, ALU.add).then_inc(s_plan, 1)
            step(n0 + 2)
            dve.tensor_reduce(tabf[:, 1, :], jump[:], AX.X, ALU.add).then_inc(s_plan, 1)
            step(n0 + 4)
            dve.scalar_tensor_tensor(out=tabf[:, 2, :], in0=tiles[:], scalar=float(P), in1=tabf[:, 1, :], op0=ALU.mult, op1=ALU.add).then_inc(s_plan, 1)
            dve.tensor_scalar(table[:, 1, :], tabf[:, 0, :], float(NE - 1), None, ALU.min)
            step(n0 + 5)
            dve.tensor_scalar(table[:, 0, :], tabf[:, 2, :], float(NE * REGION), None, ALU.min).then_inc(s_tab, 1)
            dve.wait_ge(s_tab, 1)
            dve.wait_ge(s_w1, 16 * NE)
            dve.wait_ge(s_b, 32)

            def prepare(n):
                if not n.real():
                    return
                expert = dve.value_load(table[0:1, 1, bass.ds(at(n.n), 1)], min_val=0, max_val=NE - 1)
                if not n.among_first(2):
                    dve.wait_ge(s_fh, at(2 * n.n - 2))
                dve.tensor_copy(w1f[:, n.r % 2, :], w1[:, bass.ds(expert * (ET * FF), ET * FF)]).then_inc(s_fw, 1)
                dve.wait_ge(s_ft, at(n.n + 1))
                dve.tensor_copy(xgt[n.r % 2][:], pz[:, n.r % 2, 0:E].rearrange("p (e t) -> p e t", e=ET)).then_inc(s_fxt, 1)

            def tile(t):
                prepare(t.plus(1))
                o = t.plus(-1)
                if o.real():
                    expert = dve.value_load(table[0:1, 1, bass.ds(at(o.n), 1)], min_val=0, max_val=NE - 1)
                    w = xg[:, o.r, E:E + 1]
                    if not o.first():
                        dve.wait_ge(s_fo, at(o.n))
                    dve.tensor_scalar(bw[:], b2[:, bass.ds(expert * E, E)], w, None, ALU.mult).then_inc(s_fb, 1)
                    dve.wait_ge(s_fb, at(o.n + 1))
                    dve.wait_ge(s_fy, at(o.n + 1))
                    if not o.among_first(2):
                        dve.wait_ge(s_fs, at(16 * o.n - 16))
                    dve.scalar_tensor_tensor(out=yo[:, o.r % 2, :], in0=pv[:, o.r % 2, 0:E], scalar=w, in1=bw[:],
                                             op0=ALU.mult, op1=ALU.add).then_inc(s_fo, 1)

            run_tiles(dve, tile)

            def last(u):
                if u.real():
                    c0 = 4 * u.n
                    dve.wait_ge(s_ra, at(u.n + 1))
                    dve.wait_ge(s_rl[u.r], at(32 * u.b + 32))
                    dve.tensor_tensor(tot[:, u.r, :], tot[:, u.r, :], x2in[:, u.r, :], ALU.add).then_inc(s_ln, 1)
                    dve.wait_ge(s_ln, at(c0 + 1))
                    dve.bn_stats(fst[:, u.r, :], tot[:, u.r, :]).then_inc(s_ln, 1)
                    dve.wait_ge(s_ln, at(c0 + 2))
                    dve.nop(nofuse=True)
                    dve.bn_aggr(fmv[:, u.r, :], fst[:, u.r, :]).then_inc(s_ln, 1)
                    dve.wait_ge(s_ln, at(c0 + 3))
                    dve.tensor_scalar(fve[:, u.r:u.r + 1], fmv[:, u.r, 1:2], EPS, None, ALU.add).then_inc(s_ln, 1)
                u = u.plus(-1)
                if u.real():
                    dve.wait_ge(s_lr, at(u.n + 1))
                    if not u.among_first(4):
                        dve.wait_ge(s_lo_[u.r], at(16 * u.b))
                    dve.tensor_scalar(fout[:, u.r, :], tot[:, u.r, :], fmv[:, u.r, 0:1], frs[:, u.r:u.r + 1],
                                      ALU.subtract, ALU.mult).then_inc(s_ly, 1)

            run_last(dve, last)
    return nc


def kernel(**inputs):
    import numpy as np
    import concourse.bacc as bacc
    from concourse.bass_utils import run_bass_kernel_spmd

    def units_transposed(x):
        return x.reshape(UNITS, P, ET, P).transpose(0, 3, 2, 1)

    def weight(w):
        return w.reshape(ET, P, -1).transpose(1, 0, 2)

    g = {k: np.asarray(v) for k, v in inputs.items()}
    arrays = {
        "x": g["x"].reshape(UNITS, P, E),
        "xt": units_transposed(g["x"]),
        "ct": units_transposed(g["ctx_1024"]),
        "phi": g["fside_BxSxS2_0"].reshape(UNITS, P, S),
        "wqkv": weight(np.concatenate([g["L0_attn_wq"], g["L0_attn_wk"], g["L0_attn_wv"]], 1)),
        "bqkv": np.concatenate([g["L0_attn_bq"], g["L0_attn_bk"], g["L0_attn_bv"]]),
        "wo": weight(g["L0_attn_wo"]),
        "bo": g["L0_attn_bo"],
        "gamma": g["L0_attn_gamma"],
        "beta": g["L0_attn_beta"],
        "wqx": weight(g["L0_xattn_Wq"].T),
        "wkx": weight(g["L0_xattn_Wk"].T),
        "wvx": weight(g["L0_xattn_Wv"].T),
        "bqx": g["L0_xattn_bq"].reshape(ET, P).T,
        "bkx": g["L0_xattn_bk"].reshape(ET, P).T,
        "bvx": g["L0_xattn_bv"],
        "beta_risk": g["L0_xattn_beta_risk"].reshape(1),
        "beta_prio": g["L0_xattn_beta_prio"].reshape(1),
        "beta_impl": g["L0_xattn_beta_impl"].reshape(1),
        "rw": weight(g["L0_ffn_router_w"].T),
        "w1": g["L0_ffn_w1"].transpose(0, 2, 1).reshape(NE, ET, P, FF).transpose(0, 2, 1, 3),
        "b1": g["L0_ffn_b1"].reshape(NE, FC, P).transpose(2, 0, 1),
        "w2": g["L0_ffn_w2"].transpose(0, 2, 1).reshape(NE, FC, P, E),
        "b2": g["L0_ffn_b2"].reshape(NE * E),
    }
    nc = bacc.Bacc("TRN2", target_bir_lowering=False, num_devices=1)
    tensors, sent = {}, {}
    for name, x in arrays.items():
        sent[f"in_{name}"] = np.ascontiguousarray(x)
        tensors[name] = nc.dram_tensor(f"in_{name}", x.shape, mybir.dt.from_np(x.dtype), kind="ExternalInput").ap()
    out = nc.dram_tensor("out_x", (UNITS, P, E), F32, kind="ExternalOutput").ap()
    build_decoder(nc, tensors, out)
    got = run_bass_kernel_spmd(nc, [sent], core_ids=[0])
    return got.results[0]["out_x"].reshape(B, S, E)
```

```python
from contextlib import ExitStack

import concourse.bass as bass
from concourse import mybir

F32 = mybir.dt.float32
BF16 = mybir.dt.bfloat16
FP16 = mybir.dt.float16
I32 = mybir.dt.int32
U32 = mybir.dt.uint32
ALU = mybir.AluOpType
ACT = mybir.ActivationFunctionType
AX = mybir.AxisListType

P = 128
E = 256
ET = E // P
HEADS = 4
HT = 32
G = 16
D = 16
S = 512
NJ = S // P
B = 8
T = B * S
UNITS = T // P
QB = S // P
TERMS = 6
KROWS = TERMS * D
VW = 50
NE = 8
FF = 1024
FC = FF // P
REGION = T + P
XW = E + 2
TILES = (2 * T + NE * (P - 1)) // P
DUMP = T
LAST = 4
GROUPS = T // (P * LAST)
EPS = 1e-5


class Count:

    def __init__(self, base, mul, add):
        self.base, self.mul, self.add = base, mul, add

    def __add__(self, k):
        return Count(self.base, self.mul, self.add + k)

    def __sub__(self, k):
        return self + -k

    def __mul__(self, k):
        return Count(self.base, self.mul * k, self.add * k)

    __rmul__ = __mul__


def at(count):
    if not isinstance(count, Count):
        return count
    return count.add if isinstance(count.base, int) else count.base * count.mul + count.add


class Unit:

    def __init__(self, base, off, total=UNITS):
        self.base, self.off, self.total = base, off, total
        self.r = off % 4
        self.n = Count(base, 4, off)
        self.b = Count(base, 1, off // 4)

    def plus(self, k):
        return Unit(self.base, self.off + k, self.total)

    def fixed(self):
        return isinstance(self.base, int)

    def real(self):
        return not self.fixed() or 0 <= self.off < self.total

    def among_first(self, k):
        return self.fixed() and self.off < k

    def first(self):
        return self.fixed() and self.off == 0


def build_decoder(nc, a, out):
    ctx = ExitStack()
    with ctx:
        def sb(name, shape, dt):
            return ctx.enter_context(nc.sbuf_tensor("b_" + name, shape, dt))

        def ps(name, shape, dt):
            return ctx.enter_context(nc.psum_tensor("p_" + name, shape, dt))

        def sem(name):
            return ctx.enter_context(nc.semaphore("s_" + name))

        sorted_x = nc.dram_tensor("sorted_x", (NE * REGION + P, XW), F32).ap()
        sums = nc.dram_tensor("sums", (T + P, E), F32).ap()

        identf = sb("identf", [P, P], F32)
        identb = sb("identb", [P, P], BF16)
        before = sb("before", [P, P], BF16)
        onesb = sb("onesb", [P, P], BF16)
        iota8 = sb("iota8", [P, NE], F32)
        ids = sb("ids", [P, 2], F32)
        half = sb("half", [P, 1], F32)
        bo = sb("bo", [P, E], F32)
        gamma = sb("gamma", [P, E], F32)
        beta = sb("beta", [P, E], F32)
        bqx = sb("bqx", [P, ET], F32)
        bkx = sb("bkx", [P, ET], F32)
        bvx = sb("bvx", [P, E], F32)
        betas = sb("betas", [P, 3], F32)
        coef = sb("coef", [P, 2], F32)
        rw = sb("rw", [P, ET, NE], F32)

        arena2 = sb("arena2", [P, NE * FC * E], F32)
        arena1 = sb("arena1", [P, NE * ET * FF], F32)
        arenaf = sb("arenaf", [P, 2 * ET * FF], F32)
        carved = {"b_arena2": 0, "b_arena1": 0, "b_arenaf": 0}

        def carve(words, arena=arena2):
            carved[arena.name] += words
            return arena[:, carved[arena.name] - words:carved[arena.name]]

        def square(t):
            return t.rearrange("p (e n) -> p e n", e=ET)

        prob = carve(HEADS * NJ * S)
        prob_hi = prob.bitcast(BF16)
        low = carve(HEADS * NJ * S // 2).bitcast(FP16)
        qs = [carve(HEADS * S // 2).bitcast(BF16) for _ in range(4)]
        w2 = arena2[:, :].rearrange("p (e c n) -> p e c n", e=NE, c=FC)
        wqkv = square(carve(ET * 3 * E, arena1))
        bqkv = carve(3 * E, arena1)
        q32 = carve(3 * E, arena1)
        xq = carve(G * TERMS * D // 2, arena1).bitcast(BF16).rearrange("p (g a d) -> p g a d", g=G, a=TERMS)
        xk = carve(G * TERMS * D // 2, arena1).bitcast(BF16).rearrange("p (g a d) -> p g a d", g=G, a=TERMS)
        xv = carve(G * VW // 2, arena1).bitcast(BF16).rearrange("p (g w) -> p g w", g=G)
        xt = carve(4 * E, arena1).rearrange("p (u e t) -> p u e t", u=4, e=ET)
        ct = carve(4 * E, arena1).rearrange("p (u e t) -> p u e t", u=4, e=ET)
        carve(4 * ET * FF - carved["b_arena1"], arena1)
        ks = [carve(HEADS * S // 2, arena1).bitcast(BF16) for _ in range(4)]
        vs = carve(4 * HEADS * NJ * VW // 2, arena1).bitcast(BF16).rearrange("p (u h w) -> p u h w", u=4, h=HEADS)
        wo = square(carve(ET * E, arenaf))
        wqx = square(carve(ET * E, arenaf))
        wkx = square(carve(ET * E, arenaf))
        wvx = square(carve(ET * E, arenaf))
        phs = carve(S, arenaf)
        att = carve(S, arenaf)
        p5 = carve(S, arenaf)
        p5t = carve(S, arenaf).rearrange("p (j t) -> p j t", j=QB)
        xin = sb("xin", [P, 4, E], F32)
        phi = sb("phi", [P, 4, S], F32)
        nmx = sb("nmx", [P, 2, 16], F32)
        xm = sb("xm", [P, 3, 16], BF16)
        xmr = sb("xmr", [P, 2, 16], F32)
        mrow = sb("mrow", [P, P], BF16)
        psums = sb("psums", [P, 8, D], F32)
        prec = sb("prec", [P, 8], F32)
        cx = sb("cx", [P, HEADS * 64], F32)
        cxt = sb("cxt", [P, ET, P], F32)
        xb = sb("xb", [P, 2, E], F32)
        y1 = sb("y1", [P, E], F32)
        z1 = sb("z1", [P, E], F32)
        st = sb("st", [P, 3, 6], F32)
        mv = sb("mv", [P, 3, 2], F32)
        ve = sb("ve", [P, 3], F32)
        rs = sb("rs", [P, 3], F32)
        x1 = sb("x1", [P, 2, E], F32)
        x1t = sb("x1t", [P, ET, P], F32)
        qxt = sb("qxt", [P, ET, P], F32)
        kx = sb("kx", [P, 2 * ET * S], F32)
        vx = sb("vx", [P, 2 * QB * E], F32)
        nmx5 = sb("nmx5", [P, 2], F32)
        sum5 = sb("sum5", [P, 2], F32)
        y2 = sb("y2", [P, E], F32)
        pl = sb("pl", [P, 2, 2, XW], F32)
        x2t = sb("x2t", [P, ET, P], F32)
        lg = sb("lg", [P, NE], F32)
        top = sb("top", [P, 8], F32)
        topi = sb("topi", [P, 8], U32)
        topf = sb("topf", [P, 2], F32)
        oh = sb("oh", [P, 2, NE], F32)
        chosen = sb("chosen", [P, NE], BF16)
        gate = sb("gate", [P, 3], F32)
        base = sb("base", [P, NE], F32)
        ohb = sb("ohb", [P, 2, NE], F32)
        slotf = sb("slotf", [P, 2], F32)
        slot = sb("slot", [P, 2, 2], U32)
        cnt = sb("cnt", [P, NE], F32)

        w1 = arena1
        b1 = sb("b1", [P, NE * FC], F32)
        b2 = phi[:, :, :].rearrange("p u s -> p (u s)")
        pad = sb("pad", [P, XW], F32)
        iotap = sb("iotap", [P, 2], F32)
        starts = sb("starts", [P, NE], F32)
        padf = sb("padf", [P, NE], F32)
        padto = sb("padto", [P, NE], U32)
        cnt_i = sb("cnt_i", [1, 2, NE], I32)
        plan = sb("plan", [1, 4, NE], F32)
        tiles = sb("tiles", [1, TILES], F32)
        past = kx[0:1, 0:TILES * NE].rearrange("p (t e) -> p t e", e=NE)
        jump = kx[0:1, TILES * NE:2 * TILES * NE].rearrange("p (t e) -> p t e", e=NE)
        tabf = sb("tabf", [1, 3, TILES], F32)
        table = sb("table", [1, 2, TILES], I32)
        xg = sb("xg", [P, 4, XW], F32)
        kept = sb("kept", [P, 4, 2], F32)
        w1f = arenaf[:, :].rearrange("p (a f) -> p a f", a=2)
        xgt = x1t, x2t
        hidden = [kx[:, 0:FC * P], kx[:, FC * P:2 * FC * P]]
        bw = sb("bw", [P, E], F32)
        yo = vx[:, 0:2 * E].rearrange("p (a e) -> p a e", a=2)
        tot = arena1[:, 0:GROUPS * LAST * E].rearrange("p (a e) -> p a e", e=E)
        fout = arena1[:, GROUPS * LAST * E:2 * GROUPS * LAST * E].rearrange("p (a e) -> p a e", e=E)
        fst = sb("fst", [P, 2, LAST, 6], F32)
        fmv = sb("fmv", [P, 2, LAST, 2], F32)
        fve = sb("fve", [P, 2, LAST], F32)
        frs = sb("frs", [P, 2, LAST], F32)
        fnb = sb("fnb", [P, 2, LAST], F32)

        pm = ps("pm", [P, 2, S], F32)
        pe_ = ps("pe", [P, 2, S], F32)
        pv = ps("pv", [P, 2, S], F32)
        pz = ps("pz", [P, 2, S], F32)

        def zb(bank):
            return pz[:, bank, :].bitcast(BF16)

        VEND = 2 * NJ * VW
        mrow_t = pv[:, 0, VEND:VEND + P // 2].bitcast(BF16)
        scores8 = pv[:, 1, VEND:VEND + NE]
        prefix = pv[:, 1, VEND + NE:VEND + 2 * NE]
        totals = pv[:, 1, VEND + 2 * NE:VEND + 3 * NE]

        s_wf = sem("first_weights_loaded")
        s_w = sem("weights_loaded")
        s_k = sem("constants_made")
        s_c2 = sem("coef_made")
        s_xt = [sem(f"xt_loaded{g}") for g in range(4)]
        s_xp = [sem(f"x_phi_loaded{g}") for g in range(4)]
        s_pqk = sem("proj_qk_done")
        s_pvv = sem("proj_v_done")
        s_q32 = sem("q32_written")
        s_h = sem("high_parts")
        s_r = sem("first_rest")
        s_m = sem("middle_parts")
        s_xv = sem("value_parts")
        s_rep = sem("parts_replicated")
        s_tr = sem("stack_transposed")
        s_stk = sem("stack_written")
        s_vs = [sem(f"values_moved{g}") for g in range(4)]
        s_mxq = sem("max_scores")
        s_red = sem("max_reduced")
        s_xm = sem("max_parts")
        s_mt = sem("max_transposed")
        s_mrow = sem("max_row_written")
        s_mr = [sem(f"max_rows_moved{g}") for g in range(4)]
        s_qkt = sem("exp_scores")
        s_exp = sem("exp_written")
        s_lo = sem("low_written")
        s_lod = sem("low_written_by_vector")
        s_pv = sem("values_summed")
        s_vsum = sem("value_bank_read")
        s_c = sem("context_written")
        s_ctr = sem("context_transposed")
        s_ct = sem("context_t_written")
        s_o = sem("o_proj_done")
        s_xb = sem("x_plus_bias")
        s_l1 = sem("ln1_steps")
        s_l2 = sem("ln2_steps")
        s_rs1 = sem("rstd1")
        s_rs2 = sem("rstd2")
        s_x1 = sem("x1_written")
        s_x1t = sem("x1_transposed")
        s_x1te = sem("x1t_written")
        s_qt = sem("qx_done")
        s_qte = sem("qx_written")
        s_kt = sem("kx_done")
        s_kte = sem("kx_written")
        s_vt = sem("vx_done")
        s_vte = sem("vx_written")
        s_ph = sem("phi_scaled")
        s_s = sem("cross_scores")
        s_t = sem("cross_max")
        s_e5 = sem("cross_exp")
        s_pt = sem("cross_p_transposed")
        s_pte = sem("cross_pt_written")
        s_pv5 = sem("cross_values")
        s_l5 = sem("ln5_steps")
        s_rs5 = sem("rstd5")
        s_x2 = sem("x2_written")
        s_pl2 = sem("x2_second_copy")
        s_x2d = [sem(f"x2_stored{g}") for g in range(2)]
        s_x2t = sem("x2_transposed")
        s_x2te = sem("x2t_written")
        s_rt = sem("router_done")
        s_rc = sem("choice_steps")
        s_e2 = sem("gate_exp")
        s_pf = sem("prefix_done")
        s_rd = sem("slot_steps")
        s_sc = [sem(f"rows_scattered{g}") for g in range(2)]

        s_w1 = sem("w1_loaded")
        s_w2 = sem("w2_loaded")
        s_b = sem("expert_biases_loaded")
        s_pad = sem("pad_steps")
        s_padd = sem("pads_written")
        s_plan = sem("plan_steps")
        s_tab = sem("table_written")
        s_fx = [sem(f"tile_loaded{g}") for g in range(4)]
        s_ft = sem("tile_transposed")
        s_fxt = sem("tile_t_written")
        s_fm = sem("tile_weights_kept")
        s_fw = sem("w1_fetched")
        s_fh = sem("hidden_banks")
        s_fg = sem("gelu_banks")
        s_fy = sem("expert_out")
        s_fb = sem("bias_weighted")
        s_fo = sem("result_written")
        s_fs = sem("results_scattered")
        s_rl = [sem(f"sums_loaded{g}") for g in range(GROUPS)]
        s_ln = sem("last_ln_steps")
        s_nb = sem("last_bias")
        s_lr = sem("last_rstd")
        s_ly = sem("first_half_normalised")
        s_la = sem("second_half_normalised")
        s_out = sem("output_stored")

        block = ctx.enter_context(nc.Block())

        first_loads = [(wqkv[:], a["wqkv"]), (bqkv[:], a["bqkv"].partition_broadcast(P))]
        loads = [
            (wo[:], a["wo"]), (wqx[:], a["wqx"]), (wkx[:], a["wkx"]), (wvx[:], a["wvx"]),
            (rw[:], a["rw"]), (bo[:], a["bo"].partition_broadcast(P)),
            (gamma[:], a["gamma"].partition_broadcast(P)), (beta[:], a["beta"].partition_broadcast(P)),
            (bvx[:], a["bvx"].partition_broadcast(P)), (bqx[:], a["bqx"]), (bkx[:], a["bkx"]),
            (betas[:, 0:1], a["beta_risk"].partition_broadcast(P)),
            (betas[:, 1:2], a["beta_prio"].partition_broadcast(P)),
            (betas[:, 2:3], a["beta_impl"].partition_broadcast(P)),
        ]
        NLOADS = 16 * len(loads)
        NCONST = 16

        STACKS = [8, 11, 12, 13]
        LEADS = dict(front=3, peak=2, row=1, soft=0, attn=-1, cross=-2, route=-3)

        def stages(i):
            return {name: Unit(i.base[name] if i.looped else 0, i.off + lead) for name, lead in LEADS.items()}

        def shared(u):
            return u.fixed() and UNITS - 2 <= u.off < UNITS

        class Iteration:

            def __init__(self, base, off):
                self.base, self.off, self.looped = base, off, base is not None

        def own(eng, b, most=6):
            copy = eng.alloc_register(f"stage_base{nc.next_id()}")
            eng.reg_mov(copy, b)
            return eng.snap(copy, min_val=1, max_val=most)

        def run(eng, iteration):
            for n in range(-3, 4):
                iteration(stages(Iteration(None, n)), False)
            with eng.Fori(1, 7) as b:
                base = {name: own(eng, b) for name in LEADS}
                for r in range(4):
                    iteration(stages(Iteration(base, r)), r == 0)
            for n in range(28, 35):
                iteration(stages(Iteration(None, n)), n == 28)

        def run_tiles(eng, iteration):
            for n in range(-1, 4):
                iteration(Unit(0, n, TILES))
            with eng.Fori(1, (TILES - 2) // 4) as b:
                base = own(eng, b, (TILES - 2) // 4 - 1)
                for r in range(4):
                    iteration(Unit(base, r, TILES))
            for n in range(4 * ((TILES - 2) // 4), TILES + 1):
                iteration(Unit(0, n, TILES))

        @block.sync
        def _(sp):
            def load_t(u):
                if not u.real():
                    return
                if not (u.among_first(4)):
                    sp.wait_ge(s_vt, at(u.n - 3))
                sp.dma_start(xt[:, u.r], a["xt"][bass.ds(at(u.n), 1)].rearrange("o p e t -> p (o e) t")).then_inc(s_xt[u.r], 16)
                sp.dma_start(ct[:, u.r], a["ct"][bass.ds(at(u.n), 1)].rearrange("o p e t -> p (o e) t")).then_inc(s_xt[u.r], 16)

            with nc.allow_non_contiguous_dma(reason="bias columns"):
                for dst, src in first_loads:
                    sp.dma_start(dst, src).then_inc(s_wf, 16)
                load_t(Unit(0, 0))
                for dst, src in loads:
                    sp.dma_start(dst, src).then_inc(s_w, 16)


            def iteration(st_, _):
                load_t(st_["front"].plus(1))
                i = st_["soft"]
                if i.real():
                    if not (i.among_first(4)):
                        sp.wait_ge(s_ph, at(i.n - 3))
                    sp.dma_start(xin[:, i.r], a["x"][bass.ds(at(i.n), 1)].rearrange("o t e -> (o t) e")).then_inc(s_xp[i.r], 16)
                    sp.dma_start(phi[:, i.r], a["phi"][bass.ds(at(i.n), 1)].rearrange("o t e -> (o t) e")).then_inc(s_xp[i.r], 16)
                u = st_["route"]
                if u.real():
                    sp.wait_ge(s_x2, at(u.n + 1))
                    sp.dma_start(sums[bass.ds(at(u.n) * P, P), :], pl[:, u.r % 2, 0, 0:E]).then_inc(s_x2d[u.r % 2], 16)
                u = st_["row"]
                if u.real():
                    sp.wait_ge(s_mrow, at(u.n + 1))
                    for t in range(3):
                        sp.dma_start(qs[u.r][KROWS + t:KROWS + t + 1, :].rearrange("o (m q) -> o m q", q=P),
                                     mrow[16 * t:16 * t + 16, :]).then_inc(s_mr[u.r], 16)
                u = st_["front"]
                if u.real():
                    sp.wait_ge(s_xv, at(u.n + 1))
                    sp.nop(nofuse=True)
                    if not (u.among_first(4)):
                        sp.wait_ge(s_pv, at(4 * u.n - 12))
                    for hh in range(HEADS):
                        for g4 in range(4):
                            sp.dma_start(vs[HT * g4:HT * g4 + HT, u.r, hh, :],
                                         xv[HT * hh:HT * hh + HT, 4 * g4:4 * g4 + 4, :].rearrange("p g w -> p (g w)")).then_inc(s_vs[u.r], 16)

            def load_w1(*experts):
                for e in experts:
                    sp.dma_start(w1[:, e * ET * FF:(e + 1) * ET * FF].rearrange("p (k f) -> p k f", k=ET), a["w1"][e]).then_inc(s_w1, 16)

            def load_w2(*experts):
                for e in experts:
                    sp.dma_start(w2[:, e], a["w2"][e]).then_inc(s_w2, 16)

            def with_weights(st_, entry):
                iteration(st_, entry)
                soft = st_["soft"]
                if not soft.fixed():
                    return
                if soft.off == UNITS - 3:
                    sp.wait_ge(s_vt, UNITS)
                    sp.wait_ge(s_tr, 4 * UNITS)
                    for g in range(4):
                        sp.wait_ge(s_vs[g], 256 * UNITS // 4)
                    load_w1(0, 1, 2, 3)
                if soft.off == UNITS - 2:
                    sp.wait_ge(s_mxq, 16 * UNITS)
                    sp.wait_ge(s_qkt, 16 * (UNITS - 2))
                    load_w1(4)
                    load_w2(6)
                if soft.off == UNITS - 1:
                    sp.wait_ge(s_pv, 4 * UNITS - 3)
                    load_w2(0)
                    sp.wait_ge(s_pv, 4 * UNITS - 2)
                    load_w2(1, 4)
                    sp.wait_ge(s_qkt, 16 * UNITS)
                    load_w1(5)
                    load_w2(7)
                if soft.off == UNITS:
                    sp.wait_ge(s_pv, 4 * UNITS - 1)
                    load_w2(2)
                    sp.wait_ge(s_pv, 4 * UNITS)
                    load_w1(6)
                    load_w2(3, 5)

            load_w1(7)
            sp.dma_start(b1[:].rearrange("p (e c) -> p e c", e=NE), a["b1"]).then_inc(s_b, 16)
            run(sp, with_weights)
            sp.wait_ge(s_ph, UNITS)
            sp.dma_start(b2[:], a["b2"].partition_broadcast(P)).then_inc(s_b, 16)

            def fetch(t):
                if not t.real():
                    return
                row = sp.value_load(table[0:1, 0, bass.ds(at(t.n), 1)], min_val=0, max_val=NE * REGION)
                expert = sp.value_load(table[0:1, 1, bass.ds(at(t.n), 1)], min_val=0, max_val=NE - 1)
                sp.wait_ge(s_padd, expert * 16 + 48)
                sp.nop(nofuse=True)
                if not t.among_first(4):
                    sp.wait_ge(s_fm, at(t.n - 3))
                sp.nop(nofuse=True)
                sp.dma_start(xg[:, t.r, :], sorted_x[bass.ds(row, P), :]).then_inc(s_fx[t.r], 16)

            sp.wait_ge(s_tab, 1)
            for g in range(2):
                sp.wait_ge(s_sc[g], 32 * UNITS // 2)
            fetch(Unit(0, 0, TILES))
            fetch(Unit(0, 1, TILES))
            run_tiles(sp, lambda t: fetch(t.plus(3)))

            sp.wait_ge(s_fs, 16 * TILES)
            for g in range(GROUPS):
                sp.dma_start(tot[:, g * LAST:(g + 1) * LAST, :], sums[g * LAST * P:(g + 1) * LAST * P, :].rearrange("(p a) e -> p a e", a=LAST)).then_inc(s_rl[g], 16)
            for g in range(GROUPS):
                sp.wait_ge(s_ly, g + 1)
                sp.wait_ge(s_la, g + 1)
                sp.dma_start(out[g * LAST * P:(g + 1) * LAST * P].rearrange("(p a) e -> p a e", a=LAST), fout[:, g * LAST:(g + 1) * LAST, :]).then_inc(s_out, 16)
            sp.wait_ge(s_out, 16 * GROUPS)

        @block.gpsimd
        def _(pool):
            for t, v in ((identf, 0.0), (identb, 0.0), (before, 1.0), (onesb, 1.0), (half, -0.5)):
                pool.memset(t[:], v).then_inc(s_k, 1)
            pool.memset(xv[:, :, 3 * D:3 * D + 1], 1.0).then_inc(s_k, 1)
            pool.memset(xv[:, :, 3 * D + 1:VW], 0.0).then_inc(s_k, 1)
            pool.memset(pad[:], 0.0).then_inc(s_k, 1)
            pool.iota(starts[:], [[REGION, NE]], base=0, channel_multiplier=0, allow_small_or_imprecise_dtypes=True)
            pool.iota(iotap[:], [[DUMP, 2]], base=0, channel_multiplier=1, allow_small_or_imprecise_dtypes=True)
            pool.iota(tiles[:], [[1, TILES]], base=0, channel_multiplier=0, allow_small_or_imprecise_dtypes=True)
            pool.iota(iota8[:], [[1, NE]], base=0, channel_multiplier=0, allow_small_or_imprecise_dtypes=True)
            pool.iota(cnt[:], [[REGION, NE]], base=0, channel_multiplier=0, allow_small_or_imprecise_dtypes=True)
            pool.iota(ids[:], [[0, 2]], base=0, channel_multiplier=1, allow_small_or_imprecise_dtypes=True).then_inc(s_k, 1)
            pool.wait_ge(s_k, NCONST - 3)
            for t in (identf, identb):
                pool.affine_select(out=t[:], in_=t[:], compare_op=ALU.not_equal, fill=1.0, base=0,
                                   pattern=[[-1, P]], channel_multiplier=1).then_inc(s_k, 1)
            pool.affine_select(out=before[:], in_=before[:], compare_op=ALU.is_ge, fill=0.0, base=-1,
                               pattern=[[1, P]], channel_multiplier=-1).then_inc(s_k, 1)
            pool.wait_ge(s_w, NLOADS)
            pool.wait_ge(s_k, NCONST)

            def rstd(which, ready, count, done):
                pool.wait_ge(ready, at(count))
                pool.tensor_tensor(rs[:, which:which + 1], ve[:, which:which + 1], half[:], ALU.pow).then_inc(done, 1)

            def iteration(st_, _):
                soft, attn, route = st_["soft"], st_["attn"], st_["route"]
                if route.real():
                    rstd(2, s_l5, 5 * route.n + 5, s_rs5)
                for k in range(16):
                    if k == 11 and attn.real():
                        rstd(0, s_l1, 4 * attn.n + 4, s_rs1)
                    if k == 14 and attn.real():
                        rstd(1, s_l2, 5 * attn.n + 5, s_rs2)
                    if soft.real() and not (shared(soft) and k % 2):
                        hh, j = divmod(k, NJ)
                        c0 = (hh * NJ + j) * S
                        pool.wait_ge(s_exp, at(16 * soft.n + k + 1))
                        pool.tensor_tensor(low[:, c0:c0 + S], prob[:, c0:c0 + S], prob_hi[:, 2 * c0 + 1:2 * c0 + 2 * S:2],
                                           ALU.subtract).then_inc(s_lo, 1)
                    if k == 4 and attn.real():
                        pool.wait_ge(s_xp[attn.r], at(32 * attn.b + 32))
                        if not attn.first():
                            pool.wait_ge(s_x1, at(attn.n))
                        pool.tensor_tensor(xb[:, 0, :], xin[:, attn.r, :], bo[:], ALU.add).then_inc(s_xb, 1)
                        pool.tensor_tensor(xb[:, 1, :], xin[:, attn.r, :], beta[:], ALU.add).then_inc(s_xb, 1)
                    if k == 13 and route.real():
                        pool.wait_ge(s_rd, at(7 * route.n + 7))
                        pool.wait_ge(s_pl2, at(route.n + 1))
                        g = route.r % 2
                        pool.nop(nofuse=True)
                        for c in range(2):
                            pool.indirect_dma_start(sorted_x, bass.IndirectOffsetOnAxis(ap=slot[:, g, c:c + 1], axis=0),
                                                    pl[:, g, c, :], None, bounds_check=NE * REGION + P - 1).then_inc(s_sc[g], 16)

            pool.wait_ge(s_pad, 1)
            pool.dma_start(sorted_x[NE * REGION:NE * REGION + P, :], pad[:]).then_inc(s_padd, 16)
            pool.dma_start(sums[DUMP:DUMP + P, :], pad[:, 0:E]).then_inc(s_padd, 16)
            run(pool, iteration)
            pool.wait_ge(s_pad, 3)
            for e in range(NE):
                pool.wait_ge(s_padd, 16 * (e + 2))
                pool.indirect_dma_start(sorted_x, bass.IndirectOffsetOnAxis(ap=padto[:, e:e + 1], axis=0),
                                        pad[:], None, bounds_check=NE * REGION + P - 1).then_inc(s_padd, 16)
            pool.wait_ge(s_padd, 16 * (NE + 2))
            for g in range(2):
                pool.wait_ge(s_x2d[g], 16 * UNITS // 2)

            def scatter(t):
                t = t.plus(-1)
                if t.real():
                    pool.wait_ge(s_fo, at(t.n + 1))
                    if not t.first():
                        pool.wait_ge(s_fs, at(16 * t.n))
                    pool.nop(nofuse=True)
                    pool.indirect_dma_start(sums, bass.IndirectOffsetOnAxis(ap=kept[:, t.r, 1:2].bitcast(U32), axis=0),
                                            yo[:, t.r % 2, :], None, bounds_check=T + P - 1, compute_op=ALU.add).then_inc(s_fs, 16)

            run_tiles(pool, scatter)

            for g in range(GROUPS):
                pool.wait_ge(s_ln, 3 * g + 3)
                pool.tensor_tensor(frs[:, g % 2, :], fve[:, g % 2, :], half[:].to_broadcast([P, LAST]), ALU.pow).then_inc(s_lr, 1)

        @block.tensor
        def _(pe):
            pe.wait_ge(s_wf, 32)
            pe.wait_ge(s_k, NCONST)
            read = {}

            def wait_low(u, chunks):
                if shared(u):
                    pe.wait_ge(s_lo, 16 * (UNITS - 2) + 8 * (u.off - UNITS + 2) + chunks // 2)
                    pe.wait_ge(s_lod, 8 * (u.off - UNITS + 2) + chunks // 2)
                else:
                    pe.wait_ge(s_lo, at(16 * u.n + chunks))

            def bank(z, reader, count):
                if z in read:
                    pe.wait_ge(read[z][0], at(read[z][1]))
                read[z] = (reader, count)

            def side(k, st_):
                front, peak, row, attn = st_["front"], st_["peak"], st_["row"], st_["attn"]
                cross, route = st_["cross"], st_["route"]
                if k == 0 and front.real():
                    pe.wait_ge(s_xt[front.r], at(32 * front.b + 32))
                    bank(0, s_q32, 2 * front.n + 1)
                    for e in range(ET):
                        last = nc.tensor.matmul(pz[:, 0, :], xt[:, front.r, e, :], wqkv[:, e, 0:2 * E], start=e == 0, stop=e == ET - 1)
                    last.then_inc(s_pqk, 1)
                if k == 1 and front.real():
                    bank(1, s_q32, 2 * front.n + 2)
                    for e in range(ET):
                        last = nc.tensor.matmul(pz[:, 1, 0:E], xt[:, front.r, e, :], wqkv[:, e, 2 * E:3 * E], start=e == 0, stop=e == ET - 1)
                    last.then_inc(s_pvv, 1)
                if k == 2 and cross.real():
                    pe.wait_ge(s_x1, at(cross.n + 1))
                    bank(0, s_x1te, cross.n + 1)
                    for e in range(ET):
                        last = nc.tensor.transpose(pz[:, 0, e * P:e * P + P], x1[:, cross.r % 2, e * P:e * P + P], identf[:])
                    last.then_inc(s_x1t, 1)
                if k == 5 and row.real():
                    if attn.real():
                        pe.wait_ge(s_vsum, at(2 * attn.n + 1))
                    pe.wait_ge(s_xm, at(4 * row.n + 4))
                    pe.nop(nofuse=True)
                    nc.tensor.transpose(mrow_t[0:48, :], xm[:].rearrange("p a b -> p (a b)"), identb[:]).then_inc(s_mt, 1)
                if k == 3 and route.real():
                    pe.wait_ge(s_x2, at(route.n + 1))
                    bank(1, s_x2te, route.n + 1)
                    for e in range(ET):
                        last = nc.tensor.transpose(pz[:, 1, e * P:e * P + P], pl[:, route.r % 2, 0, e * P:e * P + P], identf[:])
                    last.then_inc(s_x2t, 1)
                if k == 4 and cross.real():
                    bank(0, s_qte, cross.n + 1)
                    for m in range(ET):
                        for e in range(ET):
                            last = nc.tensor.matmul(pz[:, 0, m * P:m * P + P], wqx[:, e, m * P:m * P + P], x1t[:, e, :], start=e == 0, stop=e == ET - 1)
                    last.then_inc(s_qt, 1)
                if k == 5 and peak.real():
                    if peak.first():
                        pe.wait_ge(s_w, NLOADS)
                    bank(1, s_kte, peak.n + 1)
                    for m in range(ET):
                        for e in range(ET):
                            last = nc.tensor.matmul(pz[:, 1, m * P:m * P + P], wkx[:, e, m * P:m * P + P], ct[:, peak.r, e, :], start=e == 0, stop=e == ET - 1)
                    last.then_inc(s_kt, 1)
                if k == 6 and cross.real():
                    pe.wait_ge(s_kte, at(4 * cross.b + 4))
                    bank(0, s_t, 2 * cross.n + 1)
                    par = at(cross.b) % 2
                    for e in range(ET):
                        last = nc.tensor.matmul(pz[:, 0, :], qxt[:, e, :], kx[:, bass.ds(par * (ET * S) + e * S, S)], start=e == 0, stop=e == ET - 1)
                    last.then_inc(s_s, 1)
                if k == 7 and attn.real():
                    pe.wait_ge(s_c, at(2 * attn.n + 2))
                    bank(1, s_ct, attn.n + 1)
                    pe.nop(nofuse=True)
                    for hh in range(HEADS):
                        last = nc.tensor.transpose(pz[0:64, 1, hh * P:hh * P + P], cx[:, hh * 64:hh * 64 + 64], identf[:])
                    last.then_inc(s_ctr, 1)
                if k == 6 and route.real():
                    pe.wait_ge(s_x2te, at(route.n + 1))
                    if attn.real():
                        pe.wait_ge(s_vsum, at(2 * attn.n + 2))
                    for e in range(ET):
                        last = nc.tensor.matmul(scores8, x2t[:, e, :], rw[:, e, :], start=e == 0, stop=e == ET - 1)
                    last.then_inc(s_rt, 1)
                if k == 9 and attn.real():
                    bank(1, s_l1, 4 * attn.n + 1)
                    for e in range(ET):
                        last = nc.tensor.matmul(pz[:, 1, 0:E], cxt[:, e, :], wo[:, e, :], start=e == 0, stop=e == ET - 1)
                    last.then_inc(s_o, 1)
                if k in STACKS and front.real():
                    n, z = STACKS.index(k), k % 2
                    if n % 2 == 0:
                        pe.wait_ge(s_rep, at(2 * front.n + 1 + n // 2))
                    bank(z, s_stk, 4 * front.n + n + 1)
                    for t in range(8):
                        g = 8 * (n % 2) + t
                        group = 4 * (g % 4) + g // 4
                        last = nc.tensor.transpose(zb(z)[0:KROWS, t * P:t * P + P], (xq if n < 2 else xk)[:, group].rearrange("p a d -> p (a d)"),
                                                   identb[:])
                    last.then_inc(s_tr, 1)
                if k == 10 and cross.real():
                    pe.wait_ge(s_e5, at(cross.n + 1))
                    bank(0, s_pte, cross.n + 1)
                    for j in range(QB):
                        last = nc.tensor.transpose(pz[:, 0, j * P:j * P + P], p5[:, j * P:j * P + P], identf[:])
                    last.then_inc(s_pt, 1)
                if k == 11 and route.real():
                    pe.wait_ge(s_rc, at(8 * route.n + 8))
                    nc.tensor.matmul(prefix, before[:], chosen[:], start=True, stop=True)
                    nc.tensor.matmul(totals, onesb[:], chosen[:], start=True, stop=True).then_inc(s_pf, 1)
                if k == 14 and cross.real():
                    pe.wait_ge(s_pte, at(cross.n + 1))
                    pe.wait_ge(s_vte, at(4 * cross.b + 4))
                    bank(0, s_l5, 5 * cross.n + 2)
                    par = at(cross.b) % 2
                    for j in range(QB):
                        last = nc.tensor.matmul(pz[:, 0, 0:E], p5t[:, j, :], vx[:, bass.ds(par * (QB * E) + j * E, E)], start=j == 0, stop=j == QB - 1)
                    last.then_inc(s_pv5, 1)
                if k == 15 and peak.real():
                    bank(1, s_vte, peak.n + 1)
                    for e in range(ET):
                        last = nc.tensor.matmul(pz[:, 1, 0:E], ct[:, peak.r, e, :], wvx[:, e, :], start=e == 0, stop=e == ET - 1)
                    last.then_inc(s_vt, 1)

            def iteration(st_, entry):
                peak, soft = st_["peak"], st_["soft"]
                if entry:
                    read[0] = (s_l5, 5 * st_["cross"].plus(-1).n + 2)
                    read[1] = (s_vte, st_["peak"].plus(-1).n + 1)
                for k in range(16):
                    hh, j = divmod(k, NJ)
                    q0 = hh * S
                    if peak.real():
                        if k == 0:
                            pe.wait_ge(s_stk, at(4 * peak.n + 4))
                        if not (peak.first() and k < 2):
                            pe.wait_ge(s_red, at(16 * peak.n + k - 1))
                        nc.tensor.matmul(pm[:, k % 2, :], qs[peak.r][0:KROWS, q0 + j * P:q0 + j * P + P],
                                         ks[peak.r][0:KROWS, q0:q0 + S], start=True, stop=True).then_inc(s_mxq, 1)
                    if soft.real():
                        if k == 0:
                            pe.wait_ge(s_mr[soft.r], at(48 * soft.b + 48))
                        if not (soft.first() and k < 2):
                            pe.wait_ge(s_exp, at(16 * soft.n + k - 1))
                        nc.tensor.matmul(pe_[:, k % 2, :], ks[soft.r][0:KROWS + 3, q0 + j * P:q0 + j * P + P],
                                         qs[soft.r][0:KROWS + 3, q0:q0 + S], start=True, stop=True).then_inc(s_qkt, 1)
                    u = soft if k >= 6 else st_["attn"]
                    if u.real():
                        hv, c = divmod((k - 6) % 16, NJ)
                        if c == 0:
                            wait_low(u, 4 * hv + 4)
                            if hv == 0:
                                pe.wait_ge(s_vs[u.r], at(256 * u.b + 256))
                            if hv % 2 == 0 and not u.first():
                                pe.wait_ge(s_vsum, at(2 * u.n + hv // 2 - 1))
                            if hv == 0 and st_["row"].real():
                                pe.wait_ge(s_mrow, at(st_["row"].n + 1))
                            if hv == 2 and st_["route"].real():
                                pe.wait_ge(s_rd, at(7 * st_["route"].n + 5))
                        dst = pv[:, hv // 2, (hv % 2) * NJ * VW + c * VW:(hv % 2) * NJ * VW + c * VW + 3 * D + 1]
                        for jj in range(NJ):
                            p0 = (hv * NJ + jj) * S + c * P
                            v = vs[:, u.r, hv, jj * VW:jj * VW + 3 * D + 1]
                            nc.tensor.matmul(dst, prob_hi[:, 2 * p0 + 1:2 * p0 + 2 * P:2], v, start=jj == 0, stop=False)
                            last = nc.tensor.matmul(dst, low[:, p0:p0 + P], v, start=False, stop=jj == NJ - 1)
                        if c == NJ - 1:
                            last.then_inc(s_pv, 1)
                    side(k, st_)

            run(pe, iteration)

            pe.wait_ge(s_w2, 16 * NE)
            pe.wait_ge(s_tab, 1)

            def tile(t):
                n = t.plus(1)
                if n.real():
                    pe.wait_ge(s_fx[n.r], at(16 * n.b + 16))
                    if not n.among_first(2):
                        pe.wait_ge(s_fxt, at(n.n - 1))
                    for e in range(ET):
                        last = nc.tensor.transpose(pz[:, n.r % 2, e * P:e * P + P], xg[:, n.r, e * P:e * P + P], identf[:])
                    last.then_inc(s_ft, 1)
                if t.real():
                    hbank = (pm, pe_)[t.r % 2]
                    xT = xgt[t.r % 2]
                    pe.wait_ge(s_fxt, at(t.n + 1))
                    pe.wait_ge(s_fw, at(t.n + 1))
                    for c in range(FC):
                        if c % 4 == 0 and not t.among_first(2):
                            pe.wait_ge(s_fg, at(2 * t.n - 3 + c // 4))
                        for e in range(ET):
                            last = nc.tensor.matmul(hbank[:, c // 4, (c % 4) * P:(c % 4) * P + P],
                                                    w1f[:, t.r % 2, e * FF + c * P:e * FF + c * P + P], xT[:, e, :],
                                                    start=e == 0, stop=e == ET - 1)
                        if c % 4 == 3:
                            last.then_inc(s_fh, 1)
                o = t.plus(-1)
                if o.real():
                    expert = pe.value_load(table[0:1, 1, bass.ds(at(o.n), 1)], min_val=0, max_val=NE - 1)
                    if not o.among_first(2):
                        pe.wait_ge(s_fo, at(o.n - 1))
                    for c in range(FC):
                        if c % 4 == 0:
                            pe.wait_ge(s_fg, at(2 * o.n + 1 + c // 4))
                        last = nc.tensor.matmul(pv[:, o.r % 2, 0:E], hidden[o.r % 2][:, c * P:c * P + P],
                                                arena2[:, bass.ds(expert * (FC * E) + c * E, E)], start=c == 0, stop=c == FC - 1)
                    last.then_inc(s_fy, 1)

            run_tiles(pe, tile)

        @block.scalar
        def _(act):
            act.wait_ge(s_k, NCONST)

            def stack_evac(n, front, z):
                dst = (qs if n < 2 else ks)[front.r]
                h = n % 2
                act.wait_ge(s_tr, at(4 * front.n + n + 1))
                o = dst[0:KROWS, :].rearrange("p (h g s) -> p g h s", h=HEADS, g=G)[:, 8 * h:8 * h + 8]
                act.activation(o, zb(z)[0:KROWS, :].rearrange("p (g h s) -> p g h s", g=8, h=HEADS), ACT.Copy).then_inc(s_stk, 1)

            def side(k, st_):
                front, peak, row, attn = st_["front"], st_["peak"], st_["row"], st_["attn"]
                cross, route = st_["cross"], st_["route"]
                if k == 5 and row.real():
                    act.wait_ge(s_mt, at(row.n + 1))
                    if not row.first():
                        act.wait_ge(s_mr[row.plus(-1).r], at(48 * row.plus(-1).b + 48))
                    act.activation(mrow[0:48, :], mrow_t[0:48, :], ACT.Copy).then_inc(s_mrow, 1)
                if k == 3 and route.real():
                    act.wait_ge(s_x2, at(route.n + 1))
                    act.activation(pl[:, route.r % 2, 1, 0:E], pl[:, route.r % 2, 0, 0:E], ACT.Copy).then_inc(s_pl2, 1)
                if k == 3 and front.real():
                    act.wait_ge(s_q32, at(2 * front.n + 2))
                    if not front.first():
                        before_ = front.plus(-1)
                        act.wait_ge(s_tr, at(4 * front.n))
                        act.wait_ge(s_vs[before_.r], at(256 * before_.b + 256))
                    act.activation(xq[:, :, 0, :], q32[:, 0:E].rearrange("p (g d) -> p g d", g=G), ACT.Copy)
                    act.activation(xk[:, :, 0, :], q32[:, E:2 * E].rearrange("p (g d) -> p g d", g=G), ACT.Copy)
                    act.activation(xv[:, :, 0:D], q32[:, 2 * E:3 * E].rearrange("p (g d) -> p g d", g=G), ACT.Copy).then_inc(s_h, 1)
                if k == 2 and cross.real():
                    act.wait_ge(s_x1t, at(cross.n + 1))
                    if not cross.first():
                        act.wait_ge(s_qt, at(cross.n))
                    act.activation(x1t[:], pz[:, 0, 0:E].rearrange("p (e t) -> p e t", e=ET), ACT.Copy).then_inc(s_x1te, 1)
                if k == 6 and front.real():
                    act.wait_ge(s_r, at(front.n + 1))
                    act.activation(xq[:, :, 3, :], q32[:, 0:E].rearrange("p (g d) -> p g d", g=G), ACT.Copy)
                    act.activation(xk[:, :, 1, :], q32[:, E:2 * E].rearrange("p (g d) -> p g d", g=G), ACT.Copy)
                    act.activation(xv[:, :, D:2 * D], q32[:, 2 * E:3 * E].rearrange("p (g d) -> p g d", g=G), ACT.Copy).then_inc(s_m, 1)
                if k == 4 and route.real():
                    act.wait_ge(s_x2t, at(route.n + 1))
                    if not route.first():
                        act.wait_ge(s_rt, at(route.n))
                    act.activation(x2t[:], pz[:, 1, 0:E].rearrange("p (e t) -> p e t", e=ET), ACT.Copy).then_inc(s_x2te, 1)
                if k == 5 and cross.real():
                    act.wait_ge(s_qt, at(cross.n + 1))
                    if not cross.first():
                        act.wait_ge(s_s, at(cross.n))
                    for m in range(ET):
                        last = act.activation(qxt[:, m, :], pz[:, 0, m * P:m * P + P], ACT.Identity, bias=bqx[:, m:m + 1])
                    last.then_inc(s_qte, 1)
                if k == 6 and peak.real():
                    if peak.first():
                        act.wait_ge(s_w, NLOADS)
                    act.wait_ge(s_kt, at(peak.n + 1))
                    if not peak.among_first(8) and peak.r == 0:
                        act.wait_ge(s_s, at(4 * peak.b - 4))
                    par = at(peak.b) % 2
                    for m in range(ET):
                        last = act.activation(kx[:, bass.ds(par * (ET * S) + m * S + peak.r * P, P)], pz[:, 1, m * P:m * P + P],
                                              ACT.Identity, bias=bkx[:, m:m + 1])
                    last.then_inc(s_kte, 1)
                if k - 1 in STACKS and front.real():
                    stack_evac(STACKS.index(k - 1), front, (k - 1) % 2)
                if k == 1 and cross.real():
                    if cross.first():
                        act.wait_ge(s_c2, 2)
                    act.wait_ge(s_xp[cross.r], at(32 * cross.b + 32))
                    if not cross.first():
                        act.wait_ge(s_t, at(2 * cross.n - 1))
                    act.activation(phs[:], phi[:, cross.r, :], ACT.Copy, scale=coef[:, 1:2]).then_inc(s_ph, 1)
                if k == 8 and attn.real():
                    act.wait_ge(s_ctr, at(attn.n + 1))
                    if not attn.first():
                        act.wait_ge(s_o, at(attn.n))
                    v = pz[0:64, 1, :].rearrange("p (h e a s) -> p a e h s", h=HEADS, e=ET, a=2)
                    for par in range(2):
                        last = act.activation(cxt[64 * par:64 * par + 64].rearrange("p e (h s) -> p e h s", h=HEADS), v[:, par], ACT.Copy)
                    last.then_inc(s_ct, 1)
                if k == 10 and cross.real():
                    act.wait_ge(s_t, at(2 * cross.n + 2))
                    if not cross.first():
                        act.wait_ge(s_pt, at(cross.n))
                        act.wait_ge(s_l5, at(5 * cross.n - 3))
                    act.activation(p5[:], att[:], ACT.Exp, bias=nmx5[:, 1:2], scale=1.0 / 16, accum_out=sum5[:, 0:1]).then_inc(s_e5, 1)
                if k == 9 and route.real():
                    act.wait_ge(s_rc, at(8 * route.n + 4))
                    act.activation(gate[:, 1:2], gate[:, 0:1], ACT.Exp).then_inc(s_e2, 1)
                if k == 11 and cross.real():
                    act.wait_ge(s_pt, at(cross.n + 1))
                    if not cross.first():
                        act.wait_ge(s_pv5, at(cross.n))
                    act.activation(p5t[:], pz[:, 0, :].rearrange("p (j t) -> p j t", j=QB), ACT.Copy).then_inc(s_pte, 1)

            def iteration(st_, _):
                soft = st_["soft"]
                for k in range(16):
                    side(k, st_)
                    if soft.real():
                        hh, j = divmod(k, NJ)
                        c0 = (hh * NJ + j) * S
                        if j == 0 and not soft.first():
                            act.wait_ge(s_pv, at(4 * soft.n - 3 + hh))
                        act.wait_ge(s_qkt, at(16 * soft.n + k + 1))
                        act.activation(prob[:, c0:c0 + S], pe_[:, k % 2, :], ACT.Exp, scale=0.25).then_inc(s_exp, 1)

            run(act, iteration)

            act.wait_ge(s_tab, 1)
            act.wait_ge(s_b, 32)

            def tile(t):
                if not t.real():
                    return
                expert = act.value_load(table[0:1, 1, bass.ds(at(t.n), 1)], min_val=0, max_val=NE - 1)
                if not t.among_first(2):
                    act.wait_ge(s_fy, at(t.n - 1))
                for c in range(FC):
                    if c % 4 == 0:
                        act.wait_ge(s_fh, at(2 * t.n + 1 + c // 4))
                    last = act.activation(hidden[t.r % 2][:, c * P:c * P + P], (pm, pe_)[t.r % 2][:, c // 4, (c % 4) * P:(c % 4) * P + P],
                                          ACT.Gelu, bias=b1[:, bass.ds(expert * FC + c, 1)])
                    if c % 4 == 3:
                        last.then_inc(s_fg, 1)

            run_tiles(act, tile)

            for g in range(GROUPS):
                act.wait_ge(s_nb, g + 1)
                for u in range(LAST // 2, LAST):
                    last = act.activation(fout[:, g * LAST + u, :], tot[:, g * LAST + u, :], ACT.Identity,
                                          bias=fnb[:, g % 2, u:u + 1], scale=frs[:, g % 2, u:u + 1])
                last.then_inc(s_la, 1)

        @block.vector
        def _(dve):
            for g in range(4):
                dve.memset(ks[g][KROWS:KROWS + 3, :], 1.0).then_inc(s_k, 1)
            dve.wait_ge(s_k, NCONST)
            dve.tensor_copy(pad[:, E + 1:E + 2].bitcast(I32), iotap[:, 1:2]).then_inc(s_pad, 1)
            dve.wait_ge(s_wf, 32)

            def groups(t):
                return t.rearrange("p (g d) -> p g d", g=G)

            def stats(src, w, s, n0):
                dve.wait_ge(s, at(n0))
                dve.bn_stats(st[:, w, :], src).then_inc(s, 1)
                dve.wait_ge(s, at(n0 + 1))
                dve.nop(nofuse=True)
                dve.bn_aggr(mv[:, w, :], st[:, w, :]).then_inc(s, 1)
                dve.wait_ge(s, at(n0 + 2))
                dve.tensor_scalar(ve[:, w:w + 1], mv[:, w, 1:2], EPS, None, ALU.add).then_inc(s, 1)

            def average(q, u):
                dve.wait_ge(s_pv, at(4 * u.n + 2 * q + 2))
                v = pv[:, q, 0:8 * VW].rearrange("p (a w) -> p a w", w=VW)
                dve.tensor_reduce(psums[:], v[:, :, 0:3 * D].rearrange("p a (t d) -> p a d t", t=3), AX.X, ALU.add)
                dve.reciprocal(prec[:], v[:, :, 3 * D]).then_inc(s_vsum, 1)
                dve.wait_ge(s_vsum, at(2 * u.n + q + 1))
                if q == 0 and not u.first():
                    dve.wait_ge(s_ctr, at(u.n))
                dve.tensor_tensor(cx[:, q * P:q * P + P].rearrange("p (a d) -> p a d", d=D), psums[:],
                                  prec[:].unsqueeze(2).to_broadcast([P, 8, D]), ALU.mult).then_inc(s_c, 1)

            def prompt(k, st_):
                front, peak, row, soft, attn = st_["front"], st_["peak"], st_["row"], st_["soft"], st_["attn"]
                cross, route = st_["cross"], st_["route"]
                if k == 0 and row.first():
                    dve.wait_ge(s_w, NLOADS)
                    dve.tensor_tensor(coef[:, 0:1], betas[:, 0:1], betas[:, 1:2], ALU.add).then_inc(s_c2, 1)
                    dve.wait_ge(s_c2, 1)
                    dve.tensor_scalar(coef[:, 1:2], coef[:, 0:1], betas[:, 2:3], 16.0, ALU.subtract, ALU.mult).then_inc(s_c2, 1)
                if k == 0 and row.real():
                    dve.wait_ge(s_vt, at(row.n + 1))
                    par = at(row.b) % 2
                    dve.tensor_tensor(vx[:, bass.ds(par * (QB * E) + row.r * E, E)], pz[:, 1, 0:E], bvx[:], ALU.add).then_inc(s_vte, 1)
                if k == 0 and cross.real():
                    dve.wait_ge(s_rs2, at(cross.n + 1))
                    if not cross.among_first(2):
                        dve.wait_ge(s_x1t, at(cross.n - 1))
                    dve.tensor_scalar(x1[:, cross.r % 2, :], z1[:], mv[:, 1, 0:1], rs[:, 1:2], ALU.subtract, ALU.mult).then_inc(s_x1, 1)
                if k == 1 and front.real():
                    dve.wait_ge(s_pqk, at(front.n + 1))
                    dve.tensor_tensor(q32[:, 0:2 * E], pz[:, 0, :], bqkv[:, 0:2 * E], ALU.add).then_inc(s_q32, 1)
                if k == 2 and front.real():
                    dve.wait_ge(s_pvv, at(front.n + 1))
                    dve.tensor_tensor(q32[:, 2 * E:3 * E], pz[:, 1, 0:E], bqkv[:, 2 * E:3 * E], ALU.add).then_inc(s_q32, 1)
                if k == 2 and route.real():
                    g = route.r % 2
                    dve.wait_ge(s_rs5, at(route.n + 1))
                    if not (route.among_first(2)):
                        old = route.plus(-2)
                        uses = 2 * old.b + old.r // 2
                        dve.wait_ge(s_x2d[g], at(16 * uses + 16))
                        dve.wait_ge(s_sc[g], at(32 * uses + 32))
                    dve.tensor_scalar(pl[:, g, 0, 0:E], y2[:], mv[:, 2, 0:1], rs[:, 2:3], ALU.subtract, ALU.mult).then_inc(s_x2, 1)
                if k == 5 and front.real():
                    dve.wait_ge(s_h, at(front.n + 1))
                    for t, h in ((0, xq[:, :, 0, :]), (1, xk[:, :, 0, :]), (2, xv[:, :, 0:D])):
                        q = groups(q32[:, t * E:t * E + E])
                        last = dve.tensor_tensor(q, q, h, ALU.subtract)
                    last.then_inc(s_r, 1)
                if k == 6 and attn.real():
                    average(1, attn)
                if k == 7 and cross.real():
                    dve.wait_ge(s_s, at(cross.n + 1))
                    dve.wait_ge(s_ph, at(cross.n + 1))
                    if not cross.first():
                        dve.wait_ge(s_e5, at(cross.n))
                    dve.nop(nofuse=True)
                    dve.tensor_tensor_reduce(out=att[:], in0=pz[:, 0, :], in1=phs[:], scale=1.0, scalar=-3.0e38,
                                             op0=ALU.add, op1=ALU.max, accum_out=nmx5[:, 0:1]).then_inc(s_t, 1)
                    dve.wait_ge(s_t, at(2 * cross.n + 1))
                    dve.tensor_scalar(nmx5[:, 1:2], nmx5[:, 0:1], -1.0 / 16, None, ALU.mult).then_inc(s_t, 1)
                if k == 10 and attn.real():
                    dve.wait_ge(s_o, at(attn.n + 1))
                    dve.wait_ge(s_xb, at(2 * attn.n + 2))
                    dve.tensor_tensor(y1[:], pz[:, 1, 0:E], xb[:, 0, :], ALU.add).then_inc(s_l1, 1)
                if k == 15 and cross.real():
                    dve.wait_ge(s_l5, at(5 * cross.n + 1))
                    dve.wait_ge(s_pv5, at(cross.n + 1))
                    dve.scalar_tensor_tensor(out=y2[:], in0=pz[:, 0, 0:E], scalar=sum5[:, 1:2], in1=x1[:, cross.r % 2, :],
                                             op0=ALU.mult, op1=ALU.add).then_inc(s_l5, 1)

            def side(k, st_):
                front, peak, row, soft, attn = st_["front"], st_["peak"], st_["row"], st_["soft"], st_["attn"]
                cross, route = st_["cross"], st_["route"]
                if k == 2 and row.real():
                    c0 = 4 * row.n
                    m = nmx[:, row.r % 2, :]
                    dve.wait_ge(s_red, at(16 * row.n + 16))
                    if not row.first():
                        dve.wait_ge(s_mt, at(row.n))
                    dve.tensor_copy(xm[:, 0, :], m).then_inc(s_xm, 1)
                    dve.wait_ge(s_xm, at(c0 + 1))
                    dve.tensor_tensor(xmr[:, 0, :], m, xm[:, 0, :], ALU.subtract).then_inc(s_xm, 1)
                    dve.wait_ge(s_xm, at(c0 + 2))
                    dve.tensor_copy(xm[:, 1, :], xmr[:, 0, :]).then_inc(s_xm, 1)
                    dve.wait_ge(s_xm, at(c0 + 3))
                    dve.tensor_tensor(xm[:, 2, :], xmr[:, 0, :], xm[:, 1, :], ALU.subtract).then_inc(s_xm, 1)
                if k == 6 and front.real():
                    dve.wait_ge(s_m, at(front.n + 1))
                    dve.tensor_tensor(xv[:, :, 2 * D:3 * D], groups(q32[:, 2 * E:3 * E]), xv[:, :, D:2 * D], ALU.subtract).then_inc(s_xv, 1)
                if k == 6 and front.real():
                    dve.tensor_tensor(xq[:, :, 5, :], groups(q32[:, 0:E]), xq[:, :, 3, :], ALU.subtract)
                    dve.tensor_copy(xq[:, :, 1:3, :], xq[:, :, 0:1, :].to_broadcast([P, G, 2, D]))
                    dve.tensor_copy(xq[:, :, 4, :], xq[:, :, 3, :]).then_inc(s_rep, 1)
                if k == 9 and front.real():
                    dve.tensor_tensor(xk[:, :, 2, :], groups(q32[:, E:2 * E]), xk[:, :, 1, :], ALU.subtract)
                    dve.tensor_copy(xk[:, :, 3:5, :], xk[:, :, 0:2, :])
                    dve.tensor_copy(xk[:, :, 5, :], xk[:, :, 0, :]).then_inc(s_rep, 1)
                if k == 7 and route.real():
                    c0 = 8 * route.n
                    dve.wait_ge(s_rt, at(route.n + 1))
                    dve.tensor_copy(lg[:], scores8).then_inc(s_rc, 1)
                    dve.wait_ge(s_rc, at(c0 + 1))
                    dve.nop(nofuse=True)
                    dve.max(top[:], lg[:]).then_inc(s_rc, 1)
                    dve.wait_ge(s_rc, at(c0 + 2))
                    dve.nop(nofuse=True)
                    dve.max_index(topi[:], top[:], lg[:]).then_inc(s_rc, 1)
                    dve.tensor_tensor(gate[:, 0:1], top[:, 1:2], top[:, 0:1], ALU.subtract).then_inc(s_rc, 1)
                    dve.wait_ge(s_rc, at(c0 + 4))
                    dve.tensor_copy(topf[:], topi[:, 0:2]).then_inc(s_rc, 1)
                    dve.wait_ge(s_rc, at(c0 + 5))
                    for c in range(2):
                        dve.tensor_scalar(oh[:, c, :], iota8[:], topf[:, c:c + 1], None, ALU.is_equal).then_inc(s_rc, 1)
                    dve.wait_ge(s_rc, at(c0 + 7))
                    dve.tensor_tensor(chosen[:], oh[:, 0, :], oh[:, 1, :], ALU.add).then_inc(s_rc, 1)
                if k == 11 and attn.real():
                    stats(y1[:], 0, s_l1, 4 * attn.n + 1)
                if k == 11 and attn.real():
                    dve.wait_ge(s_l1, at(4 * attn.n + 3))
                    dve.scalar_tensor_tensor(out=z1[:], in0=y1[:], scalar=mv[:, 0, 0:1], in1=gamma[:], op0=ALU.subtract, op1=ALU.mult).then_inc(s_l2, 1)
                if k == 12 and route.real():
                    g = route.r % 2
                    c0 = 7 * route.n
                    dve.wait_ge(s_e2, at(route.n + 1))
                    dve.tensor_scalar(gate[:, 2:3], gate[:, 1:2], 1.0, None, ALU.add).then_inc(s_rd, 1)
                    dve.wait_ge(s_pf, at(route.n + 1))
                    dve.tensor_tensor(base[:], prefix, cnt[:], ALU.add).then_inc(s_rd, 1)
                    dve.wait_ge(s_rd, at(c0 + 2))
                    dve.reciprocal(pl[:, g, 0, E:E + 1], gate[:, 2:3]).then_inc(s_rd, 1)
                    for c in range(2):
                        last = dve.tensor_tensor_reduce(out=ohb[:, c, :], in0=oh[:, c, :], in1=base[:], scale=1.0, scalar=0.0,
                                                        op0=ALU.mult, op1=ALU.add, accum_out=slotf[:, c:c + 1])
                    last.then_inc(s_rd, 1)
                    dve.tensor_tensor(cnt[:], cnt[:], totals, ALU.add).then_inc(s_rd, 1)
                    dve.wait_ge(s_rd, at(c0 + 5))
                    dve.tensor_copy(slot[:, g, :], slotf[:])
                    dve.tensor_tensor(pl[:, g, 1, E:E + 1], gate[:, 1:2], pl[:, g, 0, E:E + 1], ALU.mult).then_inc(s_rd, 1)
                    dve.tensor_copy(pl[:, g, :, E + 1].bitcast(I32), ids[:]).then_inc(s_rd, 1)
                    dve.tensor_scalar(ids[:], ids[:], float(P), None, ALU.add)
                if k == 13 and attn.real():
                    c0 = 5 * attn.n
                    dve.wait_ge(s_rs1, at(attn.n + 1))
                    dve.wait_ge(s_l2, at(c0 + 1))
                    dve.scalar_tensor_tensor(out=z1[:], in0=z1[:], scalar=rs[:, 0:1], in1=xb[:, 1, :], op0=ALU.mult, op1=ALU.add).then_inc(s_l2, 1)
                    stats(z1[:], 1, s_l2, c0 + 2)
                if k == 12 and soft.real():
                    average(0, soft)
                if k == 14 and cross.real():
                    dve.wait_ge(s_e5, at(cross.n + 1))
                    dve.reciprocal(sum5[:, 1:2], sum5[:, 0:1]).then_inc(s_l5, 1)
                if k == 15 and cross.real():
                    stats(y2[:], 2, s_l5, 5 * cross.n + 2)

            def iteration(st_, _):
                peak, soft = st_["peak"], st_["soft"]
                for k in range(16):
                    prompt(k, st_)
                    if peak.real():
                        dve.wait_ge(s_mxq, at(16 * peak.n + k + 1))
                        dve.tensor_reduce(nmx[:, peak.r % 2, k:k + 1], pm[:, k % 2, :], AX.X, ALU.max, negate=True).then_inc(s_red, 1)
                    side(k, st_)
                    if soft.real() and shared(soft) and k % 2:
                        c0 = k * S
                        dve.wait_ge(s_exp, 16 * soft.off + k + 1)
                        dve.tensor_tensor(low[:, c0:c0 + S], prob[:, c0:c0 + S], prob_hi[:, 2 * c0 + 1:2 * c0 + 2 * S:2],
                                          ALU.subtract).then_inc(s_lod, 1)

            run(dve, iteration)

            dve.wait_ge(s_rd, 7 * UNITS)
            dve.tensor_scalar(padf[:], cnt[:], iotap[:, 0:1], None, ALU.add).then_inc(s_pad, 1)
            dve.wait_ge(s_pad, 2)
            dve.tensor_copy(padto[:], padf[:]).then_inc(s_pad, 1)

            def step(n):
                dve.wait_ge(s_plan, n)

            one = slice(0, 1)
            dve.tensor_tensor(plan[:, 0, :], cnt[one], starts[one], ALU.subtract).then_inc(s_plan, 1)
            step(1)
            dve.tensor_scalar(cnt_i[:, 0, :], plan[:, 0, :], float(P - 1), None, ALU.add).then_inc(s_plan, 1)
            step(2)
            dve.tensor_scalar(cnt_i[:, 1, :], cnt_i[:, 0, :], P.bit_length() - 1, None, ALU.logical_shift_right).then_inc(s_plan, 1)
            step(3)
            dve.tensor_copy(plan[:, 1, :], cnt_i[:, 1, :]).then_inc(s_plan, 1)
            step(4)
            dve.tensor_scalar(plan[:, 3, :], plan[:, 1, :], -float(P), float(REGION), ALU.mult, ALU.add).then_inc(s_plan, 1)
            dve.tensor_copy(plan[:, 2, 0:1], plan[:, 1, 0:1]).then_inc(s_plan, 1)
            for e in range(1, NE):
                step(5 + e)
                dve.tensor_tensor(plan[:, 2, e:e + 1], plan[:, 2, e - 1:e], plan[:, 1, e:e + 1], ALU.add).then_inc(s_plan, 1)
            n0 = 5 + NE
            step(n0)
            tb = tiles[:].unsqueeze(2).to_broadcast([1, TILES, NE])
            dve.tensor_tensor(past[:], tb, plan[:, 2:3, :].to_broadcast([1, TILES, NE]), ALU.is_ge).then_inc(s_plan, 1)
            step(n0 + 1)
            dve.tensor_tensor(jump[:], past[:], plan[:, 3:4, :].to_broadcast([1, TILES, NE]), ALU.mult).then_inc(s_plan, 1)
            dve.tensor_reduce(tabf[:, 0, :], past[:], AX.X, ALU.add).then_inc(s_plan, 1)
            step(n0 + 2)
            dve.tensor_reduce(tabf[:, 1, :], jump[:], AX.X, ALU.add).then_inc(s_plan, 1)
            step(n0 + 4)
            dve.scalar_tensor_tensor(out=tabf[:, 2, :], in0=tiles[:], scalar=float(P), in1=tabf[:, 1, :], op0=ALU.mult, op1=ALU.add).then_inc(s_plan, 1)
            dve.tensor_scalar(table[:, 1, :], tabf[:, 0, :], float(NE - 1), None, ALU.min)
            step(n0 + 5)
            dve.tensor_scalar(table[:, 0, :], tabf[:, 2, :], float(NE * REGION), None, ALU.min).then_inc(s_tab, 1)
            dve.wait_ge(s_tab, 1)
            dve.wait_ge(s_w1, 16 * NE)
            dve.wait_ge(s_b, 32)

            def prepare(n):
                if not n.real():
                    return
                expert = dve.value_load(table[0:1, 1, bass.ds(at(n.n), 1)], min_val=0, max_val=NE - 1)
                if not n.among_first(2):
                    dve.wait_ge(s_fh, at(2 * n.n - 2))
                dve.tensor_copy(w1f[:, n.r % 2, :], w1[:, bass.ds(expert * (ET * FF), ET * FF)]).then_inc(s_fw, 1)
                dve.wait_ge(s_ft, at(n.n + 1))
                dve.tensor_copy(xgt[n.r % 2][:], pz[:, n.r % 2, 0:E].rearrange("p (e t) -> p e t", e=ET)).then_inc(s_fxt, 1)

            def tile(t):
                prepare(t.plus(1))
                o = t.plus(-1)
                if o.real():
                    expert = dve.value_load(table[0:1, 1, bass.ds(at(o.n), 1)], min_val=0, max_val=NE - 1)
                    w = kept[:, o.r, 0:1]
                    dve.wait_ge(s_fm, at(o.n + 1))
                    if not o.first():
                        dve.wait_ge(s_fo, at(o.n))
                    dve.tensor_scalar(bw[:], b2[:, bass.ds(expert * E, E)], w, None, ALU.mult).then_inc(s_fb, 1)
                    dve.wait_ge(s_fb, at(o.n + 1))
                    dve.wait_ge(s_fy, at(o.n + 1))
                    if not o.among_first(2):
                        dve.wait_ge(s_fs, at(16 * o.n - 16))
                    dve.scalar_tensor_tensor(out=yo[:, o.r % 2, :], in0=pv[:, o.r % 2, 0:E], scalar=w, in1=bw[:],
                                             op0=ALU.mult, op1=ALU.add).then_inc(s_fo, 1)
                n = t.plus(1)
                if n.real():
                    dve.tensor_copy(kept[:, n.r, 0:1], xg[:, n.r, E:E + 1])
                    dve.tensor_copy(kept[:, n.r, 1:2].bitcast(I32), xg[:, n.r, E + 1:E + 2].bitcast(I32)).then_inc(s_fm, 1)

            run_tiles(dve, tile)

            for g in range(GROUPS + 1):
                if g < GROUPS:
                    i = g % 2
                    dve.wait_ge(s_rl[g], 16)
                    if g >= 2:
                        dve.wait_ge(s_la, g - 1)
                    for u in range(LAST):
                        last = dve.bn_stats(fst[:, i, u, :], tot[:, g * LAST + u, :])
                    last.then_inc(s_ln, 1)
                    dve.wait_ge(s_ln, 3 * g + 1)
                    for u in range(LAST):
                        last = dve.bn_aggr(fmv[:, i, u, :], fst[:, i, u, :])
                    last.then_inc(s_ln, 1)
                    dve.wait_ge(s_ln, 3 * g + 2)
                    dve.tensor_scalar(fve[:, i, :], fmv[:, i, :, 1], EPS, None, ALU.add).then_inc(s_ln, 1)
                if g > 0:
                    g, i = g - 1, (g - 1) % 2
                    dve.wait_ge(s_lr, g + 1)
                    dve.scalar_tensor_tensor(out=fnb[:, i, :], in0=fmv[:, i, :, 0], scalar=-1.0, in1=frs[:, i, :],
                                             op0=ALU.mult, op1=ALU.mult).then_inc(s_nb, 1)
                    for u in range(LAST // 2):
                        last = dve.tensor_scalar(fout[:, g * LAST + u, :], tot[:, g * LAST + u, :], fmv[:, i, u, 0:1], frs[:, i, u:u + 1],
                                                 ALU.subtract, ALU.mult)
                    last.then_inc(s_ly, 1)
    return nc


def kernel(**inputs):
    import numpy as np
    import concourse.bacc as bacc
    from concourse.bass_utils import run_bass_kernel_spmd

    def units_transposed(x):
        return x.reshape(UNITS, P, ET, P).transpose(0, 3, 2, 1)

    def weight(w):
        return w.reshape(ET, P, -1).transpose(1, 0, 2)

    g = {k: np.asarray(v) for k, v in inputs.items()}
    arrays = {
        "x": g["x"].reshape(UNITS, P, E),
        "xt": units_transposed(g["x"]),
        "ct": units_transposed(g["ctx_1024"]),
        "phi": g["fside_BxSxS2_0"].reshape(UNITS, P, S),
        "wqkv": weight(np.concatenate([g["L0_attn_wq"], g["L0_attn_wk"], g["L0_attn_wv"]], 1)),
        "bqkv": np.concatenate([g["L0_attn_bq"], g["L0_attn_bk"], g["L0_attn_bv"]]),
        "wo": weight(g["L0_attn_wo"]),
        "bo": g["L0_attn_bo"],
        "gamma": g["L0_attn_gamma"],
        "beta": g["L0_attn_beta"],
        "wqx": weight(g["L0_xattn_Wq"].T),
        "wkx": weight(g["L0_xattn_Wk"].T),
        "wvx": weight(g["L0_xattn_Wv"].T),
        "bqx": g["L0_xattn_bq"].reshape(ET, P).T,
        "bkx": g["L0_xattn_bk"].reshape(ET, P).T,
        "bvx": g["L0_xattn_bv"],
        "beta_risk": g["L0_xattn_beta_risk"].reshape(1),
        "beta_prio": g["L0_xattn_beta_prio"].reshape(1),
        "beta_impl": g["L0_xattn_beta_impl"].reshape(1),
        "rw": weight(g["L0_ffn_router_w"].T),
        "w1": g["L0_ffn_w1"].transpose(0, 2, 1).reshape(NE, ET, P, FF).transpose(0, 2, 1, 3),
        "b1": g["L0_ffn_b1"].reshape(NE, FC, P).transpose(2, 0, 1),
        "w2": g["L0_ffn_w2"].transpose(0, 2, 1).reshape(NE, FC, P, E).transpose(0, 2, 1, 3),
        "b2": g["L0_ffn_b2"].reshape(NE * E),
    }
    nc = bacc.Bacc("TRN2", target_bir_lowering=False, num_devices=1)
    tensors, sent = {}, {}
    for name, x in arrays.items():
        sent[f"in_{name}"] = np.ascontiguousarray(x)
        tensors[name] = nc.dram_tensor(f"in_{name}", x.shape, mybir.dt.from_np(x.dtype), kind="ExternalInput").ap()
    out = nc.dram_tensor("out_x", (T, E), F32, kind="ExternalOutput").ap()
    build_decoder(nc, tensors, out)
    got = run_bass_kernel_spmd(nc, [sent], core_ids=[0])
    return got.results[0]["out_x"].reshape(B, S, E)
```
